# Optimizing a Trainium2 kernel written in Bass

```python
import numpy as np
import jax
import jax.numpy as jnp

def _softmax(x, axis=-1):
    return jax.nn.softmax(x, axis=axis)

def _gelu(x):
    return jax.nn.gelu(x, approximate=True)

def _silu(x):
    return jax.nn.silu(x)

def _sigmoid(x):
    return jax.nn.sigmoid(x)

def _layernorm(x, axis=-1, eps=1e-05):
    m = jnp.mean(x, axis=axis, keepdims=True)
    v = jnp.var(x, axis=axis, keepdims=True)
    return (x - m) / jnp.sqrt(v + eps)

def _scatter_add(tgt, idx, src, axis=0):
    return tgt.at[idx].add(src)

def _segment_sum(src, seg, n):
    return jax.ops.segment_sum(src, seg, n)
kernel_name = 'mk_adj_resnorm_d1_adj_r2_6d6bda'

def setup_inputs(seed: int=0):
    np.random.seed(seed)
    _w = jnp.asarray

    def _rec_inputs():
        import jax
        import jax.numpy as jnp
        _gk = jax.random.key(seed)
        x = -0.003407 + 1.001 * jax.random.normal(jax.random.fold_in(_gk, 1), (1354, 128), jnp.float32)
        _w = (1.0 + jnp.arange(1354, dtype=jnp.float32)) ** (-0.5)
        _w = _w / _w.mean()
        _pij = jnp.clip(0.0014771 * _w[:, None] * _w[None, :], 0.0, 1.0)
        _a = jax.random.uniform(jax.random.fold_in(_gk, 2), (1354, 1354)) < _pij
        _a = jnp.logical_or(_a, jnp.swapaxes(_a, -1, -2))
        _a = jnp.logical_or(_a, jnp.eye(1354, dtype=bool))
        _af = _a.astype(jnp.float32)
        _af = _af * jax.random.uniform(jax.random.fold_in(_gk, 3), (1354, 1354), jnp.float32, 0.05, 1)
        adj = _af
        return (x, adj)
    x, adj = _rec_inputs()

    def _L0_gnn_setup():
        import jax, jax.numpy as jnp
        import numpy as np
        LN_EPS = 1e-05
        key = jax.random.key(seed)
        ks = jax.random.split(key, 6)
        N, D = (512, 128)
        return {'node_feats': jax.random.normal(ks[0], (N, D), dtype=jnp.float32), 'adj': jax.random.uniform(ks[1], (N, N), dtype=jnp.float32), 'msg_w': jax.random.normal(ks[2], (D, 2 * D), dtype=jnp.float32) * 0.05, 'msg_b': jax.random.normal(ks[3], (D,), dtype=jnp.float32) * 0.05, 'upd_w': jax.random.normal(ks[4], (D, 2 * D), dtype=jnp.float32) * 0.05, 'upd_b': jax.random.normal(ks[5], (D,), dtype=jnp.float32) * 0.05, 'ln_w': jnp.ones((D,), dtype=jnp.float32), 'ln_b': jnp.zeros((D,), dtype=jnp.float32)}
    _L0_gnn_all = _L0_gnn_setup()
    _L0_gnn_in = {k: v for k, v in _L0_gnn_all.items() if k in ('msg_w', 'msg_b', 'upd_w', 'upd_b', 'ln_w', 'ln_b')}
    del _L0_gnn_all
    return {'x': x, 'adj': adj, 'L0_gnn_msg_w': _L0_gnn_in['msg_w'], 'L0_gnn_msg_b': _L0_gnn_in['msg_b'], 'L0_gnn_upd_w': _L0_gnn_in['upd_w'], 'L0_gnn_upd_b': _L0_gnn_in['upd_b'], 'L0_gnn_ln_w': _L0_gnn_in['ln_w'], 'L0_gnn_ln_b': _L0_gnn_in['ln_b']}

def reference(x, adj, L0_gnn_msg_w, L0_gnn_msg_b, L0_gnn_upd_w, L0_gnn_upd_b, L0_gnn_ln_w, L0_gnn_ln_b):
    import jax
    import jax.numpy as jnp

    def _L0_gnn_ref(node_feats, adj, msg_w, msg_b, upd_w, upd_b, ln_w, ln_b):
        import jax, jax.numpy as jnp
        import numpy as np
        LN_EPS = 1e-05
        D = node_feats.shape[-1]
        s = node_feats @ msg_w[:, :D].T
        d = node_feats @ msg_w[:, D:].T
        messages = jax.nn.gelu(s[:, None, :] + d[None, :, :] + msg_b, approximate=False)
        aggregated = jnp.einsum('ijd,ij->id', messages, adj)
        combined = jnp.concatenate([node_feats, aggregated], axis=-1)
        new_feats = combined @ upd_w.T + upd_b
        h = jax.nn.gelu(new_feats, approximate=False) + node_feats
        mu = jnp.mean(h, axis=-1, keepdims=True)
        var = jnp.var(h, axis=-1, keepdims=True)
        return (h - mu) / jnp.sqrt(var + LN_EPS) * ln_w + ln_b
    x = _layernorm(x + _L0_gnn_ref(x, adj, L0_gnn_msg_w, L0_gnn_msg_b, L0_gnn_upd_w, L0_gnn_upd_b, L0_gnn_ln_w, L0_gnn_ln_b), axis=-1)
    return x

_drawn_inputs = setup_inputs


def setup_inputs(seed=0):
    import zlib

    import numpy as np

    out = dict(_drawn_inputs(seed))
    spreads = {'L0_gnn_ln_w': (1.0, 0.2), 'L0_gnn_ln_b': (0.0, 0.1)}
    factors = {'L0_gnn_msg_b': 3.884, 'L0_gnn_upd_b': 2.909}
    for name, (base, spread) in spreads.items():
        noise = np.random.default_rng([zlib.crc32(name.encode()), seed]).standard_normal(out[name].shape)
        drawn = base * np.exp(spread * noise) if base else spread * noise
        out[name] = jnp.asarray(drawn.astype(out[name].dtype))
    for name, factor in factors.items():
        out[name] = (out[name] * factor).astype(out[name].dtype)
    return out
```

```python
from contextlib import ExitStack

import numpy as np
import concourse.bass as bass
from concourse import mybir

F32 = mybir.dt.float32
BF16 = mybir.dt.bfloat16
F16 = mybir.dt.float16
I32 = mybir.dt.int32
U32 = mybir.dt.uint32
ALU = mybir.AluOpType
ACT = mybir.ActivationFunctionType
AX = mybir.AxisListType

P = 128
BANK = 512
SLOTS = 8
LN_EPS = 1e-5


def layer(nc, x, adj, msg_w, msg_b, upd_w, upd_b, ln_w, ln_b, out):
    N, D = x.shape
    TILES = -(-N // P)
    FULL = N // P
    TAIL = N - FULL * P
    NP = TILES * P
    SEGS_OF_TILE = [4, 2] + [1] * (TILES - 2)
    TILE_OF_SEG = [t for t in range(TILES) for _ in range(SEGS_OF_TILE[t])]
    SEGS = len(TILE_OF_SEG)
    FIRST_SEG = [TILE_OF_SEG.index(t) for t in range(TILES)]
    SPLIT_TILES = 2
    NC = -(-N // 4) * 4
    BANKS = -(-NP // BANK)
    TPB = BANK // P
    HALF = N // 2
    STREAMS = 3
    HEAVY_AT = 2
    GROUPS = [(0, 8), (8, 10), (10, 11)]


    with ExitStack() as ctx:
        def sb(name, shape, dt):
            return ctx.enter_context(nc.sbuf_tensor(name, shape, dt))

        def pb(name, shape):
            return ctx.enter_context(nc.psum_tensor(name, shape, F32))

        def sem(name):
            return ctx.enter_context(nc.semaphore(name))

        xt = sb("xt", [P, TILES, D], F32)
        xT = sb("xT", [P, NP], F32)
        wm = sb("wm", [P, 2 * D], F32)
        wu = sb("wu", [P, 2 * D], F32)
        wT = sb("wT", [P, 4, D], F32)
        msgb_bc = sb("msgb_bc", [P, D], F32)
        updb_bc = sb("updb_bc", [P, D], F32)
        lnw_bc = sb("lnw_bc", [P, D], F32)
        lnb_bc = sb("lnb_bc", [P, D], F32)
        s_rows = sb("s_rows", [P, TILES, D], F32)
        d_rows = sb("d_rows", [P, TILES, D], F32)
        dT = sb("dT", [P, NP], F32)
        adj_sb = sb("adj_sb", [P, TILES, NC], F32)
        iota1 = sb("iota1", [P, NP], F32)
        ids = sb("ids", [P, TILES], F32)
        ident = sb("ident", [P, P], F32)
        identb = sb("identb", [P, P], BF16)
        below = sb("below", [P, P], F16)
        ones16 = sb("ones16", [P, P], F16)
        ones32 = sb("ones32", [P, TILES], F32)
        zerob = sb("zerob", [1, BANK], BF16)
        top_w = sb("top_w", [P, SEGS, SLOTS], F32)
        w_flat = top_w[:, :, :].rearrange("p s k -> p (s k)")
        top_j = sb("top_j", [P, SEGS * SLOTS], U32)
        g = sb("g", [P, SEGS, SLOTS, D], F32)
        g_flat = g[:, :, :, :].rearrange("p s k d -> p (s k d)")
        nnz = sb("nnz", [P, TILES], F32)
        held = sb("held", [P, SEGS, SLOTS], F32)
        n_held = sb("n_held", [P, TILES], F32)
        heavy = sb("heavy", [P, TILES], F16)
        light = sb("light", [P, TILES], F32)
        upto = sb("upto", [P, TILES], F32)
        place = sb("place", [P, TILES], F32)
        left = sb("left", [1, 1], F32)
        over = sb("over", [1, TILES], F32)
        n_chunks = sb("n_chunks", [1, 1], F32)
        counts = sb("counts", [1, 2], I32)
        pick = sb("pick", [P, TILES, P], F32)
        pick_flat = pick[:, :, :].rearrange("p t q -> p (t q)")
        row_id = sb("row_id", [P, 1], F32)
        row_ix = sb("row_ix", [P, 1], I32)
        arow = sb("arow", [P, N], F32)
        part = sb("part", [P, 3, N], BF16)
        sTh = sb("sTh", [P, P], F32)
        msg = sb("msg", [P, 2, HALF], F32)
        sum2 = sb("sum2", [P, 2, P], F32)
        aggh = sb("aggh", [P, P], F32)
        agghT = sb("agghT", [P, D], F32)
        aggS = sb("aggS", [P, NP], F32)
        h = d_rows
        xb = sb("xb", [P, TILES, D], F32)
        y = sb("y", [P, TILES, D], F32)
        stats = sb("stats", [P, TILES, 6], F32)
        mv = sb("mv", [P, TILES, 2], F32)
        var = sb("var", [P, TILES], F32)
        sd = sb("sd", [P, TILES], F32)
        rstd = sb("rstd", [P, TILES], F32)

        aggp = pb("aggp", [P, BANKS * BANK])
        rowp = [pb(f"rowp{k}", [P, 2 * BANK]) for k in range(2)]
        small = pb("small", [P, BANK])

        def work(k):
            return rowp[k // 2][:, (k % 2) * BANK:(k % 2 + 1) * BANK]

        table = nc.dram_tensor("d_table", (NP, D), F32, kind="Internal").ap()

        passed = sem("passed")
        x_pad = sem("x_pad")
        adj_pad = sem("adj_pad")
        consts = sem("consts")
        masks = sem("masks")
        x_in = sem("x_in")
        xtail_in = sem("xtail_in")
        w_in = sem("w_in")
        vec_in = sem("vec_in")
        adj_head = [sem(f"adj_head{t}") for t in range(SPLIT_TILES)]
        adj_in = [sem(f"adj_in{u}") for u in range(STREAMS)]
        xT_ps, wT_ps, d_ps, s_ps, dT_ps = (sem(n) for n in ("xT_ps", "wT_ps", "d_ps", "s_ps", "dT_ps"))
        xT_ready, wT_ready, d_ready, s_ready, dT_ready = (
            sem(n) for n in ("xT_ready", "wT_ready", "d_ready", "s_ready", "dT_ready"))
        table_out = sem("table_out")
        xb_done = sem("xb_done")
        top_done = sem("top_done")
        found = sem("found")
        idx_ready = sem("idx_ready")
        abs_done = sem("abs_done")
        nnz_ready = sem("nnz_ready")
        list_step = sem("list_step")
        heavy_ready = sem("heavy_ready")
        places_ps = sem("places_ps")
        chunks_ready = sem("chunks_ready")
        agg_ready = sem("agg_ready")
        chunk_step = sem("chunk_step")
        pick_ready = sem("pick_ready")
        ids_ps = sem("ids_ps")
        sTh_ps = sem("sTh_ps")
        sTh_ready = sem("sTh_ready")
        row_ix_ready = sem("row_ix_ready")
        arow_in = sem("arow_in")
        parts_ready = sem("parts_ready")
        msg_ready = [sem(f"msg_ready{k}") for k in range(2)]
        rowp_ready = [sem(f"rowp_ready{k}") for k in range(2)]
        half_used = [sem(f"half_used{k}") for k in range(2)]
        aggh_ready = sem("aggh_ready")
        agghT_ps = sem("agghT_ps")
        spread_ready = sem("spread_ready")
        g_in = [sem(f"g_in{u}") for u in range(STREAMS)]
        z_ready = sem("z_ready")
        gelu_done = sem("gelu_done")
        weighted = sem("weighted")
        summed = sem("summed")
        aggS_ready = sem("aggS_ready")
        new_ps = sem("new_ps")
        new_ready = sem("new_ready")
        act_done = sem("act_done")
        fin_step = sem("fin_step")
        var_ready = sem("var_ready")
        sd_ready = sem("sd_ready")
        out_ready = sem("out_ready")
        stored = sem("stored")

        block = ctx.enter_context(nc.Block())
        CHUNK_STEPS = 6

        @block.sync
        def _(sp):
            sp.dma_start(xt[:, 0:FULL, :], x[0:FULL * P, :].rearrange("(t p) d -> p t d", p=P)).then_inc(x_in, 16)
            sp.wait_ge(x_pad, 1)
            sp.dma_start(xt[0:TAIL, FULL, :], x[FULL * P:N, :]).then_inc(xtail_in, 16)
            for t in range(SPLIT_TILES):
                sp.dma_start(adj_sb[:, t, 0:N], adj[t * P:(t + 1) * P, :]).then_inc(adj_head[t], 16)
            for u in range(STREAMS):
                t = SPLIT_TILES + u
                sp.dma_start(adj_sb[:, t, 0:N], adj[t * P:(t + 1) * P, :]).then_inc(adj_in[u], 16)
            for k in range(BANKS):
                sp.wait_ge(d_ready, k + 1)
                a, b = k * TPB, min((k + 1) * TPB, TILES)
                sp.dma_start(table[a * P:b * P, :].rearrange("(t p) d -> p t d", p=P),
                             d_rows[:, a:b, :]).then_inc(table_out, 16)
            with sp.Fori(1, 2) as i:
                for u in range(STREAMS):
                    t = i * STREAMS + SPLIT_TILES + u
                    sp.wait_ge(adj_in[u], i * 16)
                    sp.dma_start(adj_sb[:, bass.ds(t, 1), 0:N].rearrange("p o n -> p (o n)"),
                                 adj[bass.ds(t * P, P), :]).then_inc(adj_in[u], 16)
            for u in range(STREAMS):
                t = SPLIT_TILES + 2 * STREAMS + u
                rows = min(P, N - t * P)
                sp.wait_ge(adj_in[u], 32)
                if rows < P:
                    sp.wait_ge(adj_pad, 2)
                sp.dma_start(adj_sb[0:rows, t, 0:N], adj[t * P:t * P + rows, :]).then_inc(adj_in[u], 16)
            n_out = 0
            for k, (a, b) in enumerate(GROUPS):
                sp.wait_ge(out_ready, k + 1)
                f = min(b, FULL)
                if a < f:
                    sp.dma_start(out[a * P:f * P, :].rearrange("(t p) d -> p t d", p=P),
                                 y[:, a:f, :]).then_inc(stored, 16)
                    n_out += 1
                if b > FULL:
                    sp.dma_start(out[FULL * P:N, :], y[0:TAIL, FULL, :]).then_inc(stored, 16)
                    n_out += 1
            sp.wait_ge(stored, 16 * n_out)

        @block.gpsimd
        def _(pool):
            pool.iota(ids[:, :], [[P, TILES]], base=1, channel_multiplier=1,
                      allow_small_or_imprecise_dtypes=True).then_inc(consts, 1)
            pool.iota(iota1[:, :], [[1, NP]], base=1, channel_multiplier=0,
                      allow_small_or_imprecise_dtypes=True).then_inc(consts, 1)
            pool.wait_ge(table_out, 16 * BANKS)

            def gather_triples(first, last):
                for seg in range(first * STREAMS, last * STREAMS):
                    turn, u = divmod(seg, STREAMS)
                    pool.wait_ge(idx_ready, seg + 1)
                    if turn > 0:
                        pool.wait_ge(g_in[u], turn * 16 * SLOTS)
                    for k in range(SLOTS):
                        n = seg * SLOTS + k
                        pool.indirect_dma_start(g[:, seg, k, :], None, table,
                                                bass.IndirectOffsetOnAxis(top_j[:, n:n + 1], 0))\
                            .then_inc(g_in[u], 16)

            gather_triples(0, HEAVY_AT)
            pool.wait_ge(chunks_ready, 1)
            chunks = pool.value_load(counts[0:1, 0:1], min_val=1, max_val=TILES)
            with pool.Fori(0, chunks) as c:
                pool.wait_ge(row_ix_ready, c + 1)
                pool.sem_inc(passed, 1)
                pool.indirect_dma_start(arow[:, :], None, adj,
                                        bass.IndirectOffsetOnAxis(row_ix[:, 0:1], 0)).then_inc(arow_in, 16)
            gather_triples(HEAVY_AT, SEGS // STREAMS)

        @block.scalar
        def _(act):
            act.dma_start(wm[:, :], msg_w).then_inc(w_in, 16)
            act.dma_start(wu[:, :], upd_w).then_inc(w_in, 16)
            for row, vec in ((msgb_bc, msg_b), (updb_bc, upd_b), (lnw_bc, ln_w), (lnb_bc, ln_b)):
                act.dma_start(row[:, :], vec.partition_broadcast(P)).then_inc(vec_in, 16)
            for k in range(BANKS):
                w = min(BANK, NP - k * BANK)
                act.wait_ge(xT_ps, k + 1)
                nc.scalar.copy(xT[:, k * BANK:k * BANK + w], work(k)[:, 0:w]).then_inc(xT_ready, 1)
            for k in range(BANKS):
                w = min(BANK, NP - k * BANK)
                act.wait_ge(dT_ps, k + 1)
                nc.scalar.copy(dT[:, k * BANK:k * BANK + w],
                               aggp[:, k * BANK:k * BANK + w]).then_inc(dT_ready, 1)

            act.preload_act_table(ACT.Gelu)
            flat = msg[:, :, :].rearrange("p k n -> p (k n)")

            def count(t, n, tile):
                if t is None or t > 0:
                    act.wait_ge(nnz_ready, n)
                nc.scalar.activation(flat, tile, ACT.Abs).then_inc(abs_done, 1)
                act.wait_ge(abs_done, n + 1)
                col = nnz[:, t:t + 1] if t is not None else nnz[:, bass.ds(n, 1)]
                nc.scalar.activation(flat, flat, ACT.Sign, accum_out=col).then_inc(nnz_ready, 1)

            for t in range(SPLIT_TILES):
                act.wait_ge(adj_head[t], 16)
                count(t, t, adj_sb[:, t, 0:N])
            with act.Fori(0, (TILES - SPLIT_TILES) // STREAMS) as i:
                for u in range(STREAMS):
                    t = i * STREAMS + SPLIT_TILES + u
                    act.wait_ge(adj_in[u], i * 16 + 16)
                    if u == 2:
                        act.wait_ge(adj_pad, 2)
                    count(None, t, adj_sb[:, bass.ds(t, 1), 0:N].rearrange("p o n -> p (o n)"))

            act.wait_ge(nnz_ready, TILES)
            act.wait_ge(dT_ready, BANKS)
            act.wait_ge(chunks_ready, 1)
            chunks = act.value_load(counts[0:1, 0:1], min_val=1, max_val=TILES)
            with act.Fori(0, chunks) as c:
                act.wait_ge(sTh_ps, c + 1)
                nc.scalar.copy(sTh[:, :], small[:, P:2 * P]).then_inc(sTh_ready, 1)
                act.wait_ge(sTh_ready, c + 1)
                act.wait_ge(row_ix_ready, c + 1)
                act.sem_inc(passed, 1)
                rows = act.value_load(counts[0:1, 1:2], min_val=1, max_val=P)
                with act.Fori(0, rows) as r:
                    for k in range(2):
                        act.wait_ge(half_used[k], c * P + r + 1)
                        act.sem_inc(passed, 1)
                        nc.scalar.activation(msg[:, k, :], dT[:, k * HALF:(k + 1) * HALF], ACT.Gelu,
                                             bias=sTh[:, bass.ds(r, 1)]).then_inc(msg_ready[k], 1)

            def messages(first, count):
                for u in range(count):
                    seg = first + u
                    act.wait_ge(z_ready, seg + 1)
                    flat_g = g_flat[:, bass.ds(seg * SLOTS * D, SLOTS * D)]
                    nc.scalar.activation(flat_g, flat_g, ACT.Gelu).then_inc(gelu_done, 1)

            def finish(k, a, b):
                act.wait_ge(summed, FIRST_SEG[b - 1] + SEGS_OF_TILE[b - 1])
                nc.scalar.copy(aggS[:, a * P:b * P], aggp[:, a * P:b * P]).then_inc(aggS_ready, 1)
                act.wait_ge(new_ready, k + 1)
                nc.scalar.activation(h[:, a:b, :], h[:, a:b, :], ACT.Gelu).then_inc(act_done, 1)
                for n in range(2):
                    act.wait_ge(var_ready, 2 * k + n + 1)
                    nc.scalar.activation(sd[:, a:b], var[:, a:b], ACT.Sqrt).then_inc(sd_ready, 1)

            last_triple = SEGS // STREAMS - 1
            with act.Fori(0, last_triple) as i:
                messages(i * STREAMS, STREAMS)
            for k, (a, b) in enumerate(GROUPS):
                finish(k, a, b)
                if k + 1 < len(GROUPS):
                    a2, b2 = GROUPS[k + 1]
                    messages(FIRST_SEG[a2], b2 - a2)

        @block.vector
        def _(v):
            v.memset(xt[TAIL // 32 * 32:P, FULL, :], 0.0).then_inc(x_pad, 1)
            v.memset(adj_sb[:, :, N:NC], 0.0).then_inc(adj_pad, 1)
            v.memset(adj_sb[TAIL // 32 * 32:P, FULL, 0:N], 0.0).then_inc(adj_pad, 1)
            v.wait_ge(consts, 2)
            q1 = iota1[:, 0:P]
            v.tensor_scalar(ident[:, :], q1, ids[:, 0:1], None, ALU.is_equal).then_inc(masks, 1)
            v.tensor_scalar(identb[:, :], q1, ids[:, 0:1], None, ALU.is_equal).then_inc(masks, 1)
            v.tensor_scalar(below[:, :], q1, ids[:, 0:1], None, ALU.is_gt).then_inc(masks, 1)
            v.memset(ones16[:, :], 1.0).then_inc(masks, 1)
            v.memset(ones32[:, :], 1.0).then_inc(masks, 1)
            v.memset(zerob[:, :], 0.0).then_inc(masks, 1)
            v.wait_ge(wT_ps, 1)
            v.tensor_copy(wT[:, :, :].rearrange("p a d -> p (a d)"), work(3)).then_inc(wT_ready, 1)
            for k in range(BANKS):
                a, b = k * TPB, min((k + 1) * TPB, TILES)
                v.wait_ge(d_ps, k + 1)
                v.tensor_copy(d_rows[:, a:b, :].rearrange("p t d -> p (t d)"),
                              aggp[:, a * P:b * P]).then_inc(d_ready, 1)

            n_found = 0

            def top(seg, weights, step=1, first=0):
                nonlocal n_found
                tw = top_w[:, seg, :]
                tj = top_j[:, seg * SLOTS:(seg + 1) * SLOTS]
                v.max(tw, weights).then_inc(top_done, 1)
                v.wait_ge(top_done, seg + 1)
                if step == 1:
                    v.max_index(tj, tw, weights).then_inc(idx_ready, 1)
                else:
                    n_found += 1
                    v.max_index(tj, tw, weights).then_inc(found, 1)
                    v.wait_ge(found, n_found)
                    v.tensor_scalar(tj, tj, float(step), float(first), ALU.mult, ALU.add).then_inc(idx_ready, 1)

            v.wait_ge(adj_pad, 1)
            for t in range(SPLIT_TILES):
                v.wait_ge(adj_head[t], 16)
                parts = SEGS_OF_TILE[t]
                for q in range(parts):
                    seg = FIRST_SEG[t] + q
                    top(seg, adj_sb[:, t, :].rearrange("p (n q) -> p q n", q=parts)[:, q, :], parts, q)
                if t == 0:
                    v.wait_ge(vec_in, 64)
                    for k in range(BANKS):
                        a, b = k * TPB, min((k + 1) * TPB, TILES)
                        v.wait_ge(s_ps, k + 1)
                        v.tensor_tensor(s_rows[:, a:b, :],
                                        work(k)[:, 0:(b - a) * P].rearrange("p (t d) -> p t d", d=D),
                                        msgb_bc[:, :].unsqueeze(1).broadcast_to([P, b - a, D]),
                                        ALU.add).then_inc(s_ready, 1)
            for t in range(SPLIT_TILES, TILES):
                turn, u = divmod(t - SPLIT_TILES, STREAMS)
                v.wait_ge(adj_in[u], 16 * (turn + 1))
                if t == FULL:
                    v.wait_ge(adj_pad, 2)
                top(FIRST_SEG[t], adj_sb[:, t, :])

            n_list = 0

            def link(ins):
                nonlocal n_list
                n_list += 1
                ins.then_inc(list_step, 1)
                v.wait_ge(list_step, n_list)

            v.wait_ge(idx_ready, SEGS)
            link(v.tensor_scalar(held[:, :, :], top_w[:, :, :], 0.0, None, ALU.is_gt))
            for t in range(SPLIT_TILES):
                a, b = FIRST_SEG[t], FIRST_SEG[t] + SEGS_OF_TILE[t]
                v.tensor_reduce(n_held[:, t:t + 1], held[:, a:b, :].rearrange("p s k -> p (s k)"),
                                AX.X, ALU.add).then_inc(list_step, 1)
                n_list += 1
            link(v.tensor_reduce(n_held[:, SPLIT_TILES:TILES], held[:, FIRST_SEG[SPLIT_TILES]:SEGS, :],
                                 AX.X, ALU.add))
            v.wait_ge(nnz_ready, TILES)
            link(v.tensor_tensor(heavy[:, :], nnz[:, :], n_held[:, :], ALU.not_equal))
            v.tensor_tensor(light[:, :], nnz[:, :], n_held[:, :], ALU.is_equal).then_inc(heavy_ready, 1)
            v.wait_ge(heavy_ready, 1)
            for t in range(SPLIT_TILES):
                tw = top_w[:, FIRST_SEG[t]:FIRST_SEG[t] + SEGS_OF_TILE[t], :]
                v.tensor_scalar(tw, tw, light[:, t:t + 1], None, ALU.mult).then_inc(list_step, 1)
                n_list += 1
            tw = top_w[:, FIRST_SEG[SPLIT_TILES]:SEGS, :]
            link(v.tensor_tensor(tw, tw, light[:, SPLIT_TILES:TILES].unsqueeze(2).broadcast_to(
                [P, TILES - SPLIT_TILES, SLOTS]), ALU.mult))
            v.wait_ge(places_ps, 1)
            within, total = small[:, 0:TILES], small[:, 16:16 + TILES]
            link(v.tensor_tensor_scan(upto[:, :], ones32[:, :], total, 0.0, ALU.mult, ALU.add))
            link(v.tensor_tensor(place[:, :], upto[:, :], total, ALU.subtract))
            link(v.scalar_tensor_tensor(place[:, :], place[:, :], 1.0, within, ALU.add, ALU.add))
            link(v.tensor_tensor(place[:, :], place[:, :], heavy[:, :], ALU.mult))
            link(v.tensor_copy(left[:, :], upto[0:1, TILES - 1:TILES]))
            link(v.tensor_scalar(over[:, :], ids[0:1, :], -1.0, left[0:1, 0:1], ALU.add, ALU.is_lt))
            link(v.tensor_reduce(n_chunks[:, :], over[:, :], AX.X, ALU.add))
            v.tensor_scalar(counts[0:1, 0:1], n_chunks[:, :], 1.0, None, ALU.max).then_inc(chunks_ready, 1)
            v.wait_ge(chunks_ready, 1)
            chunks = v.value_load(counts[0:1, 0:1], min_val=1, max_val=TILES)
            v.wait_ge(s_ready, BANKS)
            for k in range(2):
                v.sem_inc(half_used[k], 1)
            with v.Fori(0, chunks) as c:
                def step(ins, n):
                    ins.then_inc(chunk_step, 1)
                    v.wait_ge(chunk_step, c * CHUNK_STEPS + n)

                v.wait_ge(agg_ready, c + 1)
                v.tensor_scalar(counts[0:1, 1:2], left[:, :], 1.0, float(P), ALU.max, ALU.min).then_inc(chunk_step, 1)
                v.tensor_tensor(pick[:, :, :], place[:, :].unsqueeze(2).broadcast_to([P, TILES, P]),
                                iota1[:, 0:P].unsqueeze(1).broadcast_to([P, TILES, P]),
                                ALU.is_equal).then_inc(pick_ready, 1)
                v.memset(sum2[:, :, :], 0.0).then_inc(chunk_step, 1)
                v.wait_ge(ids_ps, c + 1)
                v.wait_ge(chunk_step, c * CHUNK_STEPS + 2)
                v.tensor_copy(row_id[:, :], small[:, 40:41]).then_inc(chunk_step, 1)
                v.tensor_scalar(row_ix[:, :], small[:, 40:41], -1.0, 0.0, ALU.add, ALU.max).then_inc(row_ix_ready, 1)
                v.tensor_scalar(left[:, :], left[:, :], -float(P), None, ALU.add).then_inc(chunk_step, 1)
                v.tensor_scalar(place[:, :], place[:, :], -float(P), None, ALU.add).then_inc(chunk_step, 1)
                rows = v.value_load(counts[0:1, 1:2], min_val=1, max_val=P)
                v.wait_ge(arow_in, c * 16 + 16)
                v.tensor_copy(part[:, 0, :], arow[:, :]).then_inc(parts_ready, 1)
                v.wait_ge(parts_ready, c * 5 + 1)
                v.tensor_tensor(arow[:, :], arow[:, :], part[:, 0, :], ALU.subtract).then_inc(parts_ready, 1)
                v.wait_ge(parts_ready, c * 5 + 2)
                v.tensor_copy(part[:, 1, :], arow[:, :]).then_inc(parts_ready, 1)
                v.wait_ge(parts_ready, c * 5 + 3)
                v.tensor_tensor(part[:, 2, :], arow[:, :], part[:, 1, :], ALU.subtract).then_inc(parts_ready, 1)
                v.wait_ge(parts_ready, c * 5 + 4)
                v.wait_ge(sTh_ps, c + 1)
                v.tensor_scalar(pick_flat, iota1[:, :], row_id[:, 0:1], None,
                                ALU.is_equal).then_inc(parts_ready, 1)
                with v.Fori(0, rows) as r:
                    for k in range(2):
                        v.wait_ge(msg_ready[k], c * P + r + 1)
                        v.wait_ge(rowp_ready[k], c * P + r + 1)
                        v.scalar_tensor_tensor(msg[:, k, :], msg[:, k, :], 1.0, rowp[k][:, 0:HALF],
                                               ALU.mult, ALU.mult,
                                               accum_out=sum2[:, k, bass.ds(r, 1)]).then_inc(half_used[k], 1)
                for k in range(2):
                    v.wait_ge(half_used[k], c * P + rows + 1)
                v.tensor_tensor(aggh[:, :], sum2[:, 0, :], sum2[:, 1, :], ALU.add).then_inc(aggh_ready, 1)
                v.wait_ge(agghT_ps, c + 1)
                step(v.tensor_copy(agghT[:, :], small[:, 2 * P:3 * P]), 6)
                v.wait_ge(parts_ready, c * 5 + 5)
                v.nop().then_inc(spread_ready, 1)

            def preact(seg, tile, u, turn):
                v.wait_ge(g_in[u], turn * 16 * SLOTS + 16 * SLOTS)
                gs = g_flat[:, bass.ds(seg * SLOTS * D, SLOTS * D)].rearrange("p (k d) -> p k d", d=D)
                v.tensor_tensor(gs, gs, s_rows[:, bass.ds(tile, 1), :].broadcast_to([P, SLOTS, D]),
                                ALU.add).then_inc(z_ready, 1)

            def weigh(seg):
                v.wait_ge(gelu_done, seg + 1)
                gs = g_flat[:, bass.ds(seg * SLOTS * D, SLOTS * D)].rearrange("p (k d) -> p k d", d=D)
                ws = w_flat[:, bass.ds(seg * SLOTS, SLOTS)]
                v.tensor_tensor(gs, gs, ws.unsqueeze(2).broadcast_to([P, SLOTS, D]),
                                ALU.mult).then_inc(weighted, 1)

            n_fin = 0

            def flink(ins, wait=True):
                nonlocal n_fin
                n_fin += 1
                ins.then_inc(fin_step, 1)
                if wait:
                    v.wait_ge(fin_step, n_fin)

            def norm_stats(src, a, b, k):
                for t in range(a, b):
                    flink(v.bn_stats(stats[:, t, :], src[:, t, :]), wait=t == b - 1)
                for t in range(a, b):
                    flink(v.bn_aggr(mv[:, t, :], stats[:, t, :]), wait=t == b - 1)
                v.tensor_scalar(var[:, a:b], mv[:, a:b, 1], LN_EPS, None, ALU.add).then_inc(var_ready, 1)
                v.wait_ge(sd_ready, k + 1)
                flink(v.reciprocal(rstd[:, a:b], sd[:, a:b]))

            def finish(k, a, b):
                n = b - a
                v.wait_ge(new_ps, k + 1)
                for lo in range(0, n, TPB):
                    m = min(TPB, n - lo)
                    bank = work(2 * k + lo // TPB if k < 1 else 1 + k)
                    ins = v.tensor_tensor(h[:, a + lo:a + lo + m, :],
                                          bank[:, 0:m * P].rearrange("p (t d) -> p t d", d=D),
                                          updb_bc[:, :].unsqueeze(1).broadcast_to([P, m, D]), ALU.add)
                    if lo + m < n:
                        flink(ins)
                    else:
                        ins.then_inc(new_ready, 1)
                v.wait_ge(act_done, k + 1)
                flink(v.tensor_tensor(h[:, a:b, :], h[:, a:b, :], xt[:, a:b, :], ALU.add))
                norm_stats(h, a, b, 2 * k)
                for t in range(a, b):
                    flink(v.tensor_scalar(y[:, t, :], h[:, t, :], mv[:, t, 0:1], rstd[:, t:t + 1],
                                          ALU.subtract, ALU.mult), wait=t == b - 1)
                flink(v.tensor_tensor(y[:, a:b, :], y[:, a:b, :],
                                      lnw_bc[:, :].unsqueeze(1).broadcast_to([P, n, D]), ALU.mult))
                flink(v.tensor_tensor(y[:, a:b, :], y[:, a:b, :], xb[:, a:b, :], ALU.add))
                norm_stats(y, a, b, 2 * k + 1)
                for t in range(a, b):
                    ins = v.tensor_scalar(y[:, t, :], y[:, t, :], mv[:, t, 0:1], rstd[:, t:t + 1],
                                          ALU.subtract, ALU.mult)
                    if t < b - 1:
                        flink(ins, wait=False)
                    else:
                        flink(ins)
                v.nop().then_inc(out_ready, 1)

            v.tensor_tensor(xb[:, :, :], xt[:, :, :], lnb_bc[:, :].unsqueeze(1).broadcast_to([P, TILES, D]),
                            ALU.add).then_inc(xb_done, 1)
            v.wait_ge(xb_done, 1)
            whole = FIRST_SEG[SPLIT_TILES] // STREAMS
            for i in range(whole):
                for u in range(STREAMS):
                    preact(i * STREAMS + u, TILE_OF_SEG[i * STREAMS + u], u, i)
                for u in range(STREAMS):
                    weigh(i * STREAMS + u)
            last_triple = SEGS // STREAMS - 1
            with v.Fori(whole, last_triple) as i:
                for u in range(STREAMS):
                    preact(i * STREAMS + u, i * STREAMS + u - FIRST_SEG[SPLIT_TILES] + SPLIT_TILES, u, i)
                for u in range(STREAMS):
                    weigh(i * STREAMS + u)
            for k, (a, b) in enumerate(GROUPS):
                finish(k, a, b)
                if k + 1 < len(GROUPS):
                    for t in range(*GROUPS[k + 1]):
                        preact(FIRST_SEG[t], t, FIRST_SEG[t] % STREAMS, last_triple)
                    for t in range(*GROUPS[k + 1]):
                        weigh(FIRST_SEG[t])

        @block.tensor
        def _(pe):
            pe.wait_ge(masks, 1)
            pe.wait_ge(x_in, 16)
            for k in range(BANKS):
                a, b = k * TPB, min((k + 1) * TPB, TILES)
                if b > FULL:
                    pe.wait_ge(xtail_in, 16)
                for t in range(a, b):
                    ins = pe.transpose(work(k)[:, (t - a) * P:(t - a + 1) * P], xt[:, t, :], ident[:, :])
                ins.then_inc(xT_ps, 1)
            pe.wait_ge(w_in, 32)
            for n in range(4):
                src = wm if n < 2 else wu
                ins = pe.transpose(work(3)[:, n * P:(n + 1) * P], src[:, (n % 2) * D:(n % 2 + 1) * D], ident[:, :])
            ins.then_inc(wT_ps, 1)
            pe.wait_ge(wT_ready, 1)
            for n, dst, done in ((1, None, d_ps), (0, work, s_ps)):
                for k in range(BANKS):
                    a, b = k * TPB, min((k + 1) * TPB, TILES)
                    pe.wait_ge(xT_ready, k + 1)
                    for t in range(a, b):
                        o = aggp[:, t * P:(t + 1) * P] if dst is None else dst(k)[:, (t - a) * P:(t - a + 1) * P]
                        ins = pe.matmul(o, xT[:, t * P:(t + 1) * P], wT[:, n, :], start=True, stop=True)
                    ins.then_inc(done, 1)
            for k in range(BANKS):
                w = min(BANK, NP - k * BANK)
                pe.wait_ge(d_ready, k + 1)
                pe.matmul(aggp[:, k * BANK:k * BANK + w], wT[:, 1, :], xT[:, k * BANK:k * BANK + w],
                          start=True, stop=True).then_inc(dT_ps, 1)
            pe.wait_ge(masks, 6)
            for k in range(BANKS):
                pe.wait_ge(dT_ready, k + 1)
                ins = pe.matmul(aggp[:, k * BANK:(k + 1) * BANK], zerob[0:1, 0:P], zerob[0:1, :],
                                start=True, stop=False, skip_group_check=True)
            ins.then_inc(agg_ready, 1)

            pe.wait_ge(heavy_ready, 1)
            pe.matmul(small[:, 0:TILES], below[:, :], heavy[:, :], start=True, stop=True)
            pe.matmul(small[:, 16:16 + TILES], ones16[:, :], heavy[:, :], start=True, stop=True)\
              .then_inc(places_ps, 1)
            pe.wait_ge(chunks_ready, 1)
            chunks = pe.value_load(counts[0:1, 0:1], min_val=1, max_val=TILES)
            pe.wait_ge(s_ready, BANKS)
            with pe.Fori(0, chunks) as c:
                pe.wait_ge(pick_ready, c + 1)
                for t in range(TILES):
                    ins = pe.matmul(small[:, 40:41], pick[:, t, :], ids[:, t:t + 1],
                                    start=(t == 0), stop=(t == TILES - 1))
                ins.then_inc(ids_ps, 1)
                pe.wait_ge(row_ix_ready, c + 1)
                for t in range(TILES):
                    ins = pe.matmul(small[:, P:2 * P], s_rows[:, t, :], pick[:, t, :],
                                    start=(t == 0), stop=(t == TILES - 1))
                ins.then_inc(sTh_ps, 1)
                pe.wait_ge(parts_ready, c * 5 + 4)
                pe.sem_inc(passed, 1)
                rows = pe.value_load(counts[0:1, 1:2], min_val=1, max_val=P)
                with pe.Fori(0, rows) as r:
                    for k in range(2):
                        pe.wait_ge(half_used[k], c * P + r + 1)
                        for lo in range(0, HALF, BANK):
                            w = min(BANK, HALF - lo)
                            for n in range(3):
                                ins = pe.matmul(rowp[k][:, lo:lo + w],
                                                identb[:, bass.ds(r, 1)].broadcast_to([P, P]),
                                                part[:, n, k * HALF + lo:k * HALF + lo + w],
                                                start=(n == 0), stop=(n == 2))
                        ins.then_inc(rowp_ready[k], 1)
                pe.wait_ge(aggh_ready, c + 1)
                pe.transpose(small[:, 2 * P:3 * P], aggh[:, :], ident[:, :]).then_inc(agghT_ps, 1)
                pe.wait_ge(spread_ready, c + 1)
                for k in range(BANKS):
                    w = min(BANK, NP - k * BANK)
                    ins = pe.matmul(aggp[:, k * BANK:k * BANK + w], agghT[:, :], pick_flat[:, k * BANK:k * BANK + w],
                                    start=False, stop=False, skip_group_check=True)
                ins.then_inc(agg_ready, 1)

            def add_up(seg):
                pe.wait_ge(weighted, seg + 1)
                t = TILE_OF_SEG[seg]
                for k in range(SLOTS):
                    ins = pe.matmul(aggp[:, t * P:(t + 1) * P], g[:, seg, k, :], ident[:, :],
                                    start=False, stop=(k == SLOTS - 1), skip_group_check=True)
                ins.then_inc(summed, 1)

            seg = 0
            for k, (a, b) in enumerate(GROUPS):
                while seg < SEGS and TILE_OF_SEG[seg] < b:
                    add_up(seg)
                    seg += 1
                pe.wait_ge(aggS_ready, k + 1)
                for t in range(a, b):
                    n = t - a
                    bank = work(2 * k + n // TPB if k < 1 else 1 + k)
                    o = bank[:, (n % TPB) * P:(n % TPB + 1) * P]
                    pe.matmul(o, aggS[:, t * P:(t + 1) * P], wT[:, 3, :], start=True, stop=False)
                    ins = pe.matmul(o, xT[:, t * P:(t + 1) * P], wT[:, 2, :], start=False, stop=True)
                ins.then_inc(new_ps, 1)


_INS = ['x', 'adj', 'L0_gnn_msg_w', 'L0_gnn_msg_b', 'L0_gnn_upd_w', 'L0_gnn_upd_b', 'L0_gnn_ln_w', 'L0_gnn_ln_b']


def kernel(**inputs):
    import concourse.bacc as _bacc
    from concourse.bass_utils import run_bass_kernel_spmd as _run

    nc = _bacc.Bacc("TRN2", target_bir_lowering=False, num_devices=1)
    arrays, args = {}, []
    for name in _INS:
        a = np.ascontiguousarray(inputs[name])
        arrays[f"in_{name}_dram"] = a
        args.append(nc.dram_tensor(f"in_{name}_dram", a.shape, mybir.dt.from_np(a.dtype), kind="ExternalInput").ap())
    shape = inputs["x"].shape
    out = nc.dram_tensor("out_0_dram", shape, F32, kind="ExternalOutput").ap()
    layer(nc, *args, out)
    r = _run(nc, [arrays], core_ids=[0])
    return r.results[0]["out_0_dram"]
```

```python
from contextlib import ExitStack

import numpy as np
import concourse.bass as bass
from concourse import mybir

F32 = mybir.dt.float32
BF16 = mybir.dt.bfloat16
F16 = mybir.dt.float16
I32 = mybir.dt.int32
U32 = mybir.dt.uint32
ALU = mybir.AluOpType
ACT = mybir.ActivationFunctionType
AX = mybir.AxisListType

P = 128
BANK = 512
SLOTS = 8
LN_EPS = 1e-5


def layer(nc, x, adj, msg_w, msg_b, upd_w, upd_b, ln_w, ln_b, out):
    N, D = x.shape
    TILES = -(-N // P)
    FULL = N // P
    TAIL = N - FULL * P
    NP = TILES * P
    SEGS_OF_TILE = [4, 2] + [1] * (TILES - 2)
    TILE_OF_SEG = [t for t in range(TILES) for _ in range(SEGS_OF_TILE[t])]
    SEGS = len(TILE_OF_SEG)
    FIRST_SEG = [TILE_OF_SEG.index(t) for t in range(TILES)]
    SPLIT_TILES = 2
    NC = -(-N // 4) * 4
    BANKS = -(-NP // BANK)
    TPB = BANK // P
    HALF = N // 2
    STREAMS = 3
    CHUNK = 32
    MAX_CHUNKS = -(-N // CHUNK)
    HEAVY_AT = 5
    SCHEDULE = [("slots", 0, 5), ("heavy", 0, 0), ("slots", 5, 9), ("finish", 0, 5), ("slots", 9, 11),
                ("finish", 5, 7), ("slots", 11, 13), ("finish", 7, 9), ("slots", 13, 16), ("finish", 9, 11)]
    SLOTS_OF_SEG = [7 if t == 1 or t == TILES - 3 or t == TILES - 1 else SLOTS for t in TILE_OF_SEG]
    FIRST_SLOT = [sum(SLOTS_OF_SEG[:seg]) for seg in range(SEGS + 1)]
    PIECES = [(seg, 0, SLOTS_OF_SEG[seg]) for seg in range(SEGS - 1)]
    PIECES += [(SEGS - 1, 0, 4), (SEGS - 1, 4, SLOTS_OF_SEG[-1])]
    LANDED = [16 * sum(b - a for _, a, b in PIECES[p % STREAMS:p + 1:STREAMS]) for p in range(len(PIECES))]
    assert FIRST_SLOT[SEGS] * P <= TILES * NC
    HEAVY_AT = 5
    FINISHES = [(a, b) for what, a, b in SCHEDULE if what == "finish"]
    FIN_BANK, _n = [], 0
    for a, b in FINISHES:
        FIN_BANK.append(_n)
        _n += -(-(b - a) // TPB)

    with ExitStack() as ctx:
        def sb(name, shape, dt):
            return ctx.enter_context(nc.sbuf_tensor(name, shape, dt))

        def pb(name, shape):
            return ctx.enter_context(nc.psum_tensor(name, shape, F32))

        def sem(name):
            return ctx.enter_context(nc.semaphore(name))

        xt = sb("xt", [P, TILES, D], F32)
        xT = sb("xT", [P, NP], F32)
        wm = sb("wm", [P, 2 * D], F32)
        wu = sb("wu", [P, 2 * D], F32)
        wT = sb("wT", [P, 4, D], F32)
        msgb_bc = sb("msgb_bc", [P, D], F32)
        updb_bc = sb("updb_bc", [P, D], F32)
        lnw_bc = sb("lnw_bc", [P, D], F32)
        lnb_bc = sb("lnb_bc", [P, D], F32)
        s_rows = sb("s_rows", [P, TILES, D], F32)
        d_rows = sb("d_rows", [P, TILES, D], F32)
        dT = sb("dT", [P, NP], F32)
        adj_sb = sb("adj_sb", [P, TILES, NC], F32)
        iota1 = sb("iota1", [P, NP], F32)
        ids = sb("ids", [P, TILES], F32)
        ident = sb("ident", [P, P], F32)
        identb = sb("identb", [P, P], BF16)
        below = sb("below", [P, P], F16)
        ones16 = sb("ones16", [P, P], F16)
        ones32 = sb("ones32", [P, TILES], F32)
        sel = sb("sel", [P, CHUNK], BF16)
        zerob = sb("zerob", [1, BANK], BF16)
        top_w = sb("top_w", [P, SEGS, SLOTS], F32)
        w_flat = top_w[:, :, :].rearrange("p s k -> p (s k)")
        top_j = sb("top_j", [P, SEGS * SLOTS], U32)
        g = sb("g", [P, SEGS, SLOTS, D], F32)
        diag = adj_sb[:, :, :].rearrange("p t n -> p (t n)")[:, 0:FIRST_SLOT[SEGS] * P].rearrange(
            "p (k q) -> p k q", q=P)
        nnz = sb("nnz", [P, TILES], F32)
        held = sb("held", [P, SEGS, SLOTS], F32)
        n_held = sb("n_held", [P, TILES], F32)
        heavy = sb("heavy", [P, TILES], F16)
        light = sb("light", [P, TILES], F32)
        upto = sb("upto", [P, TILES], F32)
        place = sb("place", [P, TILES], F32)
        left = sb("left", [1, 1], F32)
        over = sb("over", [1, MAX_CHUNKS], F32)
        n_chunks = sb("n_chunks", [1, 1], F32)
        counts = sb("counts", [1, 2], I32)
        pick = sb("pick", [P, TILES, CHUNK], F32)
        picked = sb("picked", [P, TILES, CHUNK], F32)
        id_sum = sb("id_sum", [P, CHUNK], F32)
        id_rep = sb("id_rep", [P, P // CHUNK, CHUNK], F32)
        spread = sb("spread", [CHUNK, NP], F32)
        row_id = sb("row_id", [P, 1], F32)
        row_ix = sb("row_ix", [P, 1], I32)
        arow = sb("arow", [P, N], F32)
        part = sb("part", [P, N], BF16)
        sTh = sb("sTh", [P, CHUNK], F32)
        msg = sb("msg", [P, 2, N], F32)
        sum2 = sb("sum2", [P, 2, CHUNK], F32)
        aggh = sb("aggh", [P, CHUNK], F32)
        agghT = sb("agghT", [CHUNK, D], F32)
        aggS = sb("aggS", [P, NP], F32)
        h = d_rows
        xb = sb("xb", [P, TILES, D], F32)
        y = sb("y", [P, TILES, D], F32)
        stats = sb("stats", [P, TILES, 6], F32)
        mv = sb("mv", [P, TILES, 2], F32)
        var = sb("var", [P, TILES], F32)
        sd = sb("sd", [P, TILES], F32)
        rstd = sb("rstd", [P, TILES], F32)

        aggp = pb("aggp", [P, BANKS * BANK])
        rowp = [pb(f"rowp{k}", [P, 2 * BANK]) for k in range(2)]
        small = pb("small", [P, BANK])

        def work(k):
            return rowp[k // 2][:, (k % 2) * BANK:(k % 2 + 1) * BANK]

        table = nc.dram_tensor("d_table", (NP, D), F32, kind="Internal").ap()

        passed = sem("passed")
        x_pad = sem("x_pad")
        adj_pad = sem("adj_pad")
        consts = sem("consts")
        masks = sem("masks")
        x_in = [sem(f"x_in{k}") for k in range(BANKS)]
        xtail_in = sem("xtail_in")
        w_in = sem("w_in")
        vec_in = sem("vec_in")
        adj_head = [sem(f"adj_head{t}") for t in range(SPLIT_TILES)]
        adj_in = [sem(f"adj_in{u}") for u in range(STREAMS)]
        xT_ps, wT_ps, d_ps, s_ps, dT_ps = (sem(n) for n in ("xT_ps", "wT_ps", "d_ps", "s_ps", "dT_ps"))
        wT_ready, d_ready, s_ready, dT_ready = (sem(n) for n in ("wT_ready", "d_ready", "s_ready", "dT_ready"))
        xT_ready = [sem(f"xT_ready{k}") for k in range(BANKS)]
        table_out = sem("table_out")
        xb_done = sem("xb_done")
        sel_half = sem("sel_half")
        top_done = sem("top_done")
        found = sem("found")
        idx_ready = sem("idx_ready")
        cleared = sem("cleared")
        abs_done = sem("abs_done")
        nnz_ready = sem("nnz_ready")
        list_step = sem("list_step")
        heavy_ready = sem("heavy_ready")
        places_ps = sem("places_ps")
        chunks_ready = sem("chunks_ready")
        agg_ready = sem("agg_ready")
        chunk_step = sem("chunk_step")
        pick_ready = sem("pick_ready")
        ids_ps = sem("ids_ps")
        sTh_ps = sem("sTh_ps")
        sTh_ready = sem("sTh_ready")
        row_ix_ready = sem("row_ix_ready")
        arow_in = sem("arow_in")
        parts_ready = sem("parts_ready")
        part1_ready = sem("part1_ready")
        msg_ready = sem("msg_ready")
        rowp_ready = [sem(f"rowp_ready{k}") for k in range(2)]
        half_used = [sem(f"half_used{k}") for k in range(2)]
        aggh_ready = sem("aggh_ready")
        agghT_ps = sem("agghT_ps")
        spread_ready = sem("spread_ready")
        agghT_ready = sem("agghT_ready")
        id_summed = sem("id_summed")
        id_rep_ready = sem("id_rep_ready")
        g_in = [sem(f"g_in{u}") for u in range(STREAMS)]
        prefilled = sem("prefilled")
        gelu_done = sem("gelu_done")
        diag_ready = sem("diag_ready")
        summed = sem("summed")
        aggS_ready = sem("aggS_ready")
        new_ps = sem("new_ps")
        new_ready = sem("new_ready")
        act_done = sem("act_done")
        fin_step = sem("fin_step")
        var_ready = sem("var_ready")
        sd_ready = sem("sd_ready")
        out_ready = sem("out_ready")
        stored = sem("stored")

        block = ctx.enter_context(nc.Block())
        PREP_STEPS, SPLIT_STEPS = 6, 5

        @block.sync
        def _(sp):
            for k in range(BANKS):
                a, b = k * TPB, min((k + 1) * TPB, FULL)
                sp.dma_start(xt[:, a:b, :], x[a * P:b * P, :].rearrange("(t p) d -> p t d", p=P)).then_inc(x_in[k], 16)
            sp.wait_ge(x_pad, 1)
            sp.dma_start(xt[0:TAIL, FULL, :], x[FULL * P:N, :]).then_inc(xtail_in, 16)
            for t in range(SPLIT_TILES):
                sp.dma_start(adj_sb[:, t, 0:N], adj[t * P:(t + 1) * P, :]).then_inc(adj_head[t], 16)
            for k in range(BANKS):
                sp.wait_ge(d_ready, k + 1)
                a, b = k * TPB, min((k + 1) * TPB, TILES)
                sp.dma_start(table[a * P:b * P, :].rearrange("(t p) d -> p t d", p=P),
                             d_rows[:, a:b, :]).then_inc(table_out, 16)
            for u in range(STREAMS):
                t = SPLIT_TILES + u
                sp.dma_start(adj_sb[:, t, 0:N], adj[t * P:(t + 1) * P, :]).then_inc(adj_in[u], 16)
            with sp.Fori(1, 2) as i:
                for u in range(STREAMS):
                    t = i * STREAMS + SPLIT_TILES + u
                    sp.wait_ge(adj_in[u], i * 16)
                    sp.dma_start(adj_sb[:, bass.ds(t, 1), 0:N].rearrange("p o n -> p (o n)"),
                                 adj[bass.ds(t * P, P), :]).then_inc(adj_in[u], 16)
            for u in range(STREAMS):
                t = SPLIT_TILES + 2 * STREAMS + u
                rows = min(P, N - t * P)
                sp.wait_ge(adj_in[u], 32)
                if rows < P:
                    sp.wait_ge(adj_pad, 2)
                sp.dma_start(adj_sb[0:rows, t, 0:N], adj[t * P:t * P + rows, :]).then_inc(adj_in[u], 16)
            n_out = 0
            for k, (a, b) in enumerate(FINISHES):
                sp.wait_ge(out_ready, k + 1)
                f = min(b, FULL)
                if a < f:
                    sp.dma_start(out[a * P:f * P, :].rearrange("(t p) d -> p t d", p=P),
                                 y[:, a:f, :]).then_inc(stored, 16)
                    n_out += 1
                if b > FULL:
                    sp.dma_start(out[FULL * P:N, :], y[0:TAIL, FULL, :]).then_inc(stored, 16)
                    n_out += 1
            sp.wait_ge(stored, 16 * n_out)

        @block.gpsimd
        def _(pool):
            pool.iota(ids[:, :], [[P, TILES]], base=1, channel_multiplier=1,
                      allow_small_or_imprecise_dtypes=True).then_inc(consts, 1)
            for a, b in ((0, P), (P, NP)):
                pool.iota(iota1[:, a:b], [[1, b - a]], base=a + 1, channel_multiplier=0,
                          allow_small_or_imprecise_dtypes=True).then_inc(consts, 1)
            pool.wait_ge(table_out, 16 * BANKS)

            def gather(first, last):
                for p in range(first, last):
                    seg, lo, hi = PIECES[p]
                    u = p % STREAMS
                    pool.wait_ge(idx_ready, seg + 1)
                    pool.wait_ge(prefilled, seg + 1)
                    if p >= STREAMS:
                        pool.wait_ge(g_in[u], LANDED[p - STREAMS])
                    for k in range(lo, hi):
                        n = seg * SLOTS + k
                        pool.indirect_dma_start(g[:, seg, k, :], None, table,
                                                bass.IndirectOffsetOnAxis(top_j[:, n:n + 1], 0),
                                                compute_op=ALU.add).then_inc(g_in[u], 16)

            gather(0, HEAVY_AT)
            pool.wait_ge(chunks_ready, 1)
            chunks = pool.value_load(counts[0:1, 0:1], min_val=1, max_val=MAX_CHUNKS)
            with pool.Fori(0, chunks) as c:
                pool.wait_ge(row_ix_ready, c + 1)
                pool.sem_inc(passed, 1)
                pool.indirect_dma_start(arow[:, :], None, adj,
                                        bass.IndirectOffsetOnAxis(row_ix[:, 0:1], 0)).then_inc(arow_in, 16)
            gather(HEAVY_AT, len(PIECES))

        @block.scalar
        def _(act):
            act.dma_start(wm[:, :], msg_w).then_inc(w_in, 16)
            act.dma_start(wu[:, :], upd_w).then_inc(w_in, 16)
            for row, vec in ((msgb_bc, msg_b), (updb_bc, upd_b), (lnw_bc, ln_w), (lnb_bc, ln_b)):
                act.dma_start(row[:, :], vec.partition_broadcast(P)).then_inc(vec_in, 16)
            for k in range(0, BANKS, 2):
                w = min(BANK, NP - k * BANK)
                act.wait_ge(xT_ps, k + 1)
                nc.scalar.copy(xT[:, k * BANK:k * BANK + w], work(k)[:, 0:w]).then_inc(xT_ready[k], 1)
            for k in range(BANKS):
                a, b = k * TPB, min((k + 1) * TPB, TILES)
                act.wait_ge(d_ps, k + 1)
                nc.scalar.copy(d_rows[:, a:b, :].rearrange("p t d -> p (t d)"),
                               aggp[:, a * P:b * P]).then_inc(d_ready, 1)
            act.preload_act_table(ACT.Gelu)

            def prefill(first, last):
                for seg in range(first, last):
                    t = TILE_OF_SEG[seg]
                    act.wait_ge(s_ready, t // TPB + 1)
                    nc.scalar.copy(g[:, seg, 0:SLOTS_OF_SEG[seg], :], s_rows[:, t, :].unsqueeze(1).broadcast_to(
                        [P, SLOTS_OF_SEG[seg], D])).then_inc(prefilled, 1)

            scratch = [msg[:, 0, :], msg[:, 1, :], y[:, :, :].rearrange("p t d -> p (t d)")[:, 0:N]]

            def count(u, n, col):
                act.wait_ge(abs_done, n + 1)
                nc.scalar.activation(scratch[u], scratch[u], ACT.Sign, accum_out=col).then_inc(nnz_ready, 1)

            for t in range(SPLIT_TILES):
                act.wait_ge(adj_head[t], 16)
                nc.scalar.activation(scratch[t], adj_sb[:, t, 0:N], ACT.Abs).then_inc(abs_done, 1)
            for t in range(SPLIT_TILES):
                count(t, t, nnz[:, t:t + 1])
            prefill(0, FIRST_SEG[1])
            for k in range(BANKS):
                w = min(BANK, NP - k * BANK)
                act.wait_ge(dT_ps, k + 1)
                nc.scalar.copy(dT[:, k * BANK:k * BANK + w],
                               aggp[:, k * BANK:k * BANK + w]).then_inc(dT_ready, 1)
            act.wait_ge(nnz_ready, SPLIT_TILES)
            with act.Fori(0, (TILES - SPLIT_TILES) // STREAMS) as i:
                for u in range(STREAMS + 1):
                    t = i * STREAMS + SPLIT_TILES + u
                    if u < STREAMS:
                        act.wait_ge(adj_in[u], i * 16 + 16)
                        if u == 2:
                            act.wait_ge(adj_pad, 2)
                        if u == 0:
                            act.wait_ge(nnz_ready, t)
                            act.sem_inc(passed, 1)
                        nc.scalar.activation(scratch[u], adj_sb[:, bass.ds(t, 1), 0:N].rearrange("p o n -> p (o n)"),
                                             ACT.Abs).then_inc(abs_done, 1)
                    if u > 0:
                        act.wait_ge(abs_done, t)
                        act.sem_inc(passed, 1)
                        nc.scalar.activation(scratch[u - 1], scratch[u - 1], ACT.Sign,
                                             accum_out=nnz[:, bass.ds(t - 1, 1)]).then_inc(nnz_ready, 1)
            prefill(FIRST_SEG[1], SEGS)

            def slots(first, last):
                for p in range(first, last):
                    seg, lo, hi = PIECES[p]
                    act.wait_ge(g_in[p % STREAMS], LANDED[p])
                    gs = g[:, seg, lo:hi, :].rearrange("p k d -> p (k d)")
                    nc.scalar.activation(gs, gs, ACT.Gelu).then_inc(gelu_done, 1)

            def prepare(c):
                act.wait_ge(sTh_ps, c + 1)
                nc.scalar.copy(sTh[:, :], small[:, P:P + CHUNK]).then_inc(sTh_ready, 1)

            def heavy_rows():
                chunks = act.value_load(counts[0:1, 0:1], min_val=1, max_val=MAX_CHUNKS)
                with act.Fori(0, chunks) as c:
                    q = slice(CHUNK, 2 * CHUNK)
                    act.wait_ge(parts_ready, c * SPLIT_STEPS + 2)
                    nc.scalar.copy(part[q, :], arow[q, :]).then_inc(part1_ready, 1)
                    act.wait_ge(sTh_ready, c + 1)
                    act.sem_inc(passed, 1)
                    rows = act.value_load(counts[0:1, 1:2], min_val=1, max_val=CHUNK)
                    with act.Fori(0, rows) as r:
                        act.wait_ge(half_used[1], c * CHUNK + r + 1)
                        act.sem_inc(passed, 1)
                        nc.scalar.activation(msg[:, bass.ds(r % 2, 1), :].rearrange("p o n -> p (o n)"),
                                             dT[:, 0:N], ACT.Gelu, bias=sTh[:, bass.ds(r, 1)]).then_inc(msg_ready, 1)
                    with act.If(c + 1 < chunks):
                        prepare(c + 1)
                    act.end_ifs()

            def finish(k, a, b):
                act.wait_ge(summed, sum(TILE_OF_SEG[seg] < b for seg, _, _ in PIECES))
                nc.scalar.copy(aggS[:, a * P:b * P], aggp[:, a * P:b * P]).then_inc(aggS_ready, 1)
                act.wait_ge(new_ready, k + 1)
                nc.scalar.activation(h[:, a:b, :], h[:, a:b, :], ACT.Gelu).then_inc(act_done, 1)
                act.preload_act_table(ACT.Sqrt)
                for n in range(2):
                    act.wait_ge(var_ready, 2 * k + n + 1)
                    nc.scalar.activation(sd[:, a:b], var[:, a:b], ACT.Sqrt).then_inc(sd_ready, 1)
                if k < len(FINISHES) - 1:
                    act.preload_act_table(ACT.Gelu)

            act.wait_ge(nnz_ready, TILES)
            act.wait_ge(chunks_ready, 1)
            prepare(0)
            for what, a, b in SCHEDULE:
                if what == "slots":
                    slots(a, b)
                elif what == "heavy":
                    act.wait_ge(dT_ready, BANKS)
                    heavy_rows()
                else:
                    finish(FINISHES.index((a, b)), a, b)

        @block.vector
        def _(v):
            v.memset(xt[TAIL // 32 * 32:P, FULL, :], 0.0).then_inc(x_pad, 1)
            v.memset(adj_sb[:, :, N:NC], 0.0).then_inc(adj_pad, 1)
            v.memset(adj_sb[TAIL // 32 * 32:P, FULL, 0:N], 0.0).then_inc(adj_pad, 1)
            v.wait_ge(consts, 2)
            q1 = iota1[:, 0:P]
            v.tensor_scalar(ident[:, :], q1, ids[:, 0:1], None, ALU.is_equal).then_inc(masks, 1)
            v.tensor_scalar(identb[:, :], q1, ids[:, 0:1], None, ALU.is_equal).then_inc(masks, 1)
            v.tensor_scalar(below[:, :], q1, ids[:, 0:1], None, ALU.is_gt).then_inc(masks, 1)
            v.memset(ones16[:, :], 1.0).then_inc(masks, 1)
            v.memset(ones32[:, :], 1.0).then_inc(masks, 1)
            v.memset(zerob[:, :], 0.0).then_inc(masks, 1)
            v.wait_ge(masks, 2)
            v.tensor_tensor(sel[:, :], identb[:, 0:CHUNK], identb[:, CHUNK:2 * CHUNK], ALU.add).then_inc(sel_half, 1)
            v.wait_ge(sel_half, 1)
            v.tensor_tensor(sel[:, :], sel[:, :], identb[:, 2 * CHUNK:3 * CHUNK], ALU.add).then_inc(masks, 1)
            v.wait_ge(wT_ps, 1)
            v.tensor_copy(wT[:, :, :].rearrange("p a d -> p (a d)"), work(3)).then_inc(wT_ready, 1)
            v.wait_ge(xT_ps, 2)
            v.tensor_copy(xT[:, BANK:2 * BANK], work(1)).then_inc(xT_ready[1], 1)

            n_found = 0

            def top(seg, weights, step=1, first=0):
                nonlocal n_found
                tw = top_w[:, seg, :]
                tj = top_j[:, seg * SLOTS:(seg + 1) * SLOTS]
                v.max(tw, weights).then_inc(top_done, 1)
                v.wait_ge(top_done, seg + 1)
                if step == 1:
                    v.max_index(tj, tw, weights).then_inc(idx_ready, 1)
                else:
                    n_found += 1
                    v.max_index(tj, tw, weights).then_inc(found, 1)
                    v.wait_ge(found, n_found)
                    v.tensor_scalar(tj, tj, float(step), float(first), ALU.mult, ALU.add).then_inc(idx_ready, 1)
                if SLOTS_OF_SEG[seg] < SLOTS:
                    v.wait_ge(idx_ready, seg + 1)
                    v.memset(top_w[:, seg, SLOTS_OF_SEG[seg]:SLOTS], 0.0).then_inc(cleared, 1)

            v.wait_ge(adj_pad, 1)
            for t in range(SPLIT_TILES):
                v.wait_ge(adj_head[t], 16)
                parts = SEGS_OF_TILE[t]
                for q in range(parts):
                    seg = FIRST_SEG[t] + q
                    top(seg, adj_sb[:, t, :].rearrange("p (n q) -> p q n", q=parts)[:, q, :], parts, q)
                if t == 0:
                    v.wait_ge(vec_in, 64)
                    for k in range(BANKS):
                        a, b = k * TPB, min((k + 1) * TPB, TILES)
                        v.wait_ge(s_ps, k + 1)
                        v.tensor_tensor(s_rows[:, a:b, :],
                                        work(k)[:, 0:(b - a) * P].rearrange("p (t d) -> p t d", d=D),
                                        msgb_bc[:, :].unsqueeze(1).broadcast_to([P, b - a, D]),
                                        ALU.add).then_inc(s_ready, 1)
            for t in range(SPLIT_TILES, TILES):
                turn, u = divmod(t - SPLIT_TILES, STREAMS)
                v.wait_ge(adj_in[u], 16 * (turn + 1))
                if t == FULL:
                    v.wait_ge(adj_pad, 2)
                top(FIRST_SEG[t], adj_sb[:, t, :])

            n_list = 0

            def link(ins):
                nonlocal n_list
                n_list += 1
                ins.then_inc(list_step, 1)
                v.wait_ge(list_step, n_list)

            v.wait_ge(idx_ready, SEGS)
            v.wait_ge(cleared, sum(k < SLOTS for k in SLOTS_OF_SEG))
            link(v.tensor_scalar(held[:, :, :], top_w[:, :, :], 0.0, None, ALU.is_gt))
            for t in range(SPLIT_TILES):
                a, b = FIRST_SEG[t], FIRST_SEG[t] + SEGS_OF_TILE[t]
                v.tensor_reduce(n_held[:, t:t + 1], held[:, a:b, :].rearrange("p s k -> p (s k)"),
                                AX.X, ALU.add).then_inc(list_step, 1)
                n_list += 1
            link(v.tensor_reduce(n_held[:, SPLIT_TILES:TILES], held[:, FIRST_SEG[SPLIT_TILES]:SEGS, :],
                                 AX.X, ALU.add))
            v.wait_ge(nnz_ready, TILES)
            link(v.tensor_tensor(heavy[:, :], nnz[:, :], n_held[:, :], ALU.not_equal))
            v.tensor_tensor(light[:, :], nnz[:, :], n_held[:, :], ALU.is_equal).then_inc(heavy_ready, 1)
            v.wait_ge(heavy_ready, 1)
            for t in range(SPLIT_TILES):
                tw = top_w[:, FIRST_SEG[t]:FIRST_SEG[t] + SEGS_OF_TILE[t], :]
                v.tensor_scalar(tw, tw, light[:, t:t + 1], None, ALU.mult).then_inc(list_step, 1)
                n_list += 1
            tw = top_w[:, FIRST_SEG[SPLIT_TILES]:SEGS, :]
            link(v.tensor_tensor(tw, tw, light[:, SPLIT_TILES:TILES].unsqueeze(2).broadcast_to(
                [P, TILES - SPLIT_TILES, SLOTS]), ALU.mult))
            v.wait_ge(places_ps, 1)
            within, total = small[:, 0:TILES], small[:, 16:16 + TILES]
            link(v.tensor_tensor_scan(upto[:, :], ones32[:, :], total, 0.0, ALU.mult, ALU.add))
            link(v.tensor_tensor(place[:, :], upto[:, :], total, ALU.subtract))
            link(v.scalar_tensor_tensor(place[:, :], place[:, :], 1.0, within, ALU.add, ALU.add))
            link(v.tensor_tensor(place[:, :], place[:, :], heavy[:, :], ALU.mult))
            link(v.tensor_copy(left[:, :], upto[0:1, TILES - 1:TILES]))
            link(v.tensor_scalar(over[:, :], iota1[0:1, 0:MAX_CHUNKS], -1.0, float(CHUNK), ALU.add, ALU.mult))
            link(v.tensor_scalar(over[:, :], over[:, :], left[0:1, 0:1], None, ALU.is_lt))
            link(v.tensor_reduce(n_chunks[:, :], over[:, :], AX.X, ALU.add))
            v.tensor_scalar(counts[0:1, 0:1], n_chunks[:, :], 1.0, None, ALU.max).then_inc(chunks_ready, 1)
            v.wait_ge(chunks_ready, 1)
            chunks = v.value_load(counts[0:1, 0:1], min_val=1, max_val=MAX_CHUNKS)
            v.wait_ge(s_ready, BANKS)
            v.wait_ge(consts, 3)
            for k in range(2):
                v.sem_inc(half_used[k], 2)

            def prepare(c):
                base = c * PREP_STEPS
                v.wait_ge(agg_ready, c + 1)
                v.tensor_scalar(counts[0:1, 1:2], left[:, :], 1.0, float(CHUNK), ALU.max, ALU.min).then_inc(chunk_step, 1)
                v.tensor_tensor(pick[:, :, :], place[:, :].unsqueeze(2).broadcast_to([P, TILES, CHUNK]),
                                iota1[:, 0:CHUNK].unsqueeze(1).broadcast_to([P, TILES, CHUNK]),
                                ALU.is_equal).then_inc(pick_ready, 1)
                v.memset(sum2[:, :, :], 0.0).then_inc(chunk_step, 1)
                v.wait_ge(pick_ready, c + 1)
                v.tensor_tensor(picked[:, :, :], pick[:, :, :],
                                ids[:, :].unsqueeze(2).broadcast_to([P, TILES, CHUNK]), ALU.mult).then_inc(chunk_step, 1)
                v.wait_ge(chunk_step, base + 3)
                v.tensor_reduce(id_sum[:, :], picked[:, :, :].rearrange("p t q -> p q t"),
                                AX.X, ALU.add).then_inc(id_summed, 1)
                v.wait_ge(id_summed, c + 1)
                v.tensor_copy(id_rep[:, :, :], id_sum[:, :].unsqueeze(1).broadcast_to(
                    [P, P // CHUNK, CHUNK])).then_inc(id_rep_ready, 1)
                v.tensor_scalar(left[:, :], left[:, :], -float(CHUNK), None, ALU.add).then_inc(chunk_step, 1)
                v.tensor_scalar(place[:, :], place[:, :], -float(CHUNK), None, ALU.add).then_inc(chunk_step, 1)
                v.wait_ge(ids_ps, c + 1)
                v.tensor_copy(row_id[:, :], small[:, 40:41]).then_inc(chunk_step, 1)
                v.tensor_scalar(row_ix[:, :], small[:, 40:41], -1.0, 0.0, ALU.add, ALU.max).then_inc(row_ix_ready, 1)

            def heavy_rows():
                with v.Fori(0, chunks) as c:
                    base = c * SPLIT_STEPS
                    two = slice(2 * CHUNK, P)
                    v.wait_ge(chunk_step, c * PREP_STEPS + PREP_STEPS)
                    v.sem_inc(passed, 1)
                    rows = v.value_load(counts[0:1, 1:2], min_val=1, max_val=CHUNK)
                    v.tensor_scalar(spread[:, :], iota1[0:CHUNK, :], row_id[0:CHUNK, 0:1], None,
                                    ALU.is_equal).then_inc(spread_ready, 1)
                    v.wait_ge(arow_in, c * 16 + 16)
                    v.tensor_copy(part[:, :], arow[:, :]).then_inc(parts_ready, 1)
                    v.wait_ge(parts_ready, base + 1)
                    v.tensor_tensor(arow[:, :], arow[:, :], part[:, :], ALU.subtract).then_inc(parts_ready, 1)
                    v.wait_ge(parts_ready, base + 2)
                    v.tensor_copy(part[two, :], arow[two, :]).then_inc(parts_ready, 1)
                    v.wait_ge(parts_ready, base + 3)
                    v.tensor_tensor(part[two, :], arow[two, :], part[two, :], ALU.subtract).then_inc(parts_ready, 1)
                    v.wait_ge(part1_ready, c + 1)
                    v.wait_ge(parts_ready, base + 4)
                    v.sem_inc(parts_ready, 1)
                    with v.Fori(0, rows) as r:
                        for k in range(2):
                            if k == 0:
                                v.wait_ge(msg_ready, c * CHUNK + r + 1)
                            v.wait_ge(rowp_ready[k], c * CHUNK + r + 1)
                            half = msg[:, bass.ds(r % 2, 1), k * HALF:(k + 1) * HALF].rearrange("p o n -> p (o n)")
                            v.scalar_tensor_tensor(half, half, 1.0, rowp[k][:, 0:HALF], ALU.mult, ALU.mult,
                                                   accum_out=sum2[:, k, bass.ds(r, 1)]).then_inc(half_used[k], 1)
                    for k in range(2):
                        v.wait_ge(half_used[k], c * CHUNK + rows + 2)
                    v.tensor_tensor(aggh[:, :], sum2[:, 0, :], sum2[:, 1, :], ALU.add).then_inc(aggh_ready, 1)
                    v.wait_ge(agghT_ps, c + 1)
                    v.tensor_copy(agghT[:, :], small[0:CHUNK, 2 * P:3 * P]).then_inc(agghT_ready, 1)
                    with v.If(c + 1 < chunks):
                        prepare(c + 1)
                    v.end_ifs()

            def diags(first, last):
                for seg in range(first, last):
                    n = SLOTS_OF_SEG[seg]
                    v.tensor_tensor(diag[:, FIRST_SLOT[seg]:FIRST_SLOT[seg] + n, :],
                                    ident[:, :].unsqueeze(1).broadcast_to([P, n, P]),
                                    top_w[:, seg, 0:n].unsqueeze(2).broadcast_to([P, n, P]),
                                    ALU.mult).then_inc(diag_ready, 1)

            n_fin = 0

            def flink(ins, wait=True):
                nonlocal n_fin
                n_fin += 1
                ins.then_inc(fin_step, 1)
                if wait:
                    v.wait_ge(fin_step, n_fin)

            def norm_stats(src, a, b, k):
                for t in range(a, b):
                    flink(v.bn_stats(stats[:, t, :], src[:, t, :]), wait=t == b - 1)
                for t in range(a, b):
                    flink(v.bn_aggr(mv[:, t, :], stats[:, t, :]), wait=t == b - 1)
                v.tensor_scalar(var[:, a:b], mv[:, a:b, 1], LN_EPS, None, ALU.add).then_inc(var_ready, 1)
                v.wait_ge(sd_ready, k + 1)
                flink(v.reciprocal(rstd[:, a:b], sd[:, a:b]))

            def finish(k, a, b):
                n = b - a
                v.wait_ge(new_ps, k + 1)
                for lo in range(0, n, TPB):
                    m = min(TPB, n - lo)
                    bank = work((FIN_BANK[k] + lo // TPB) % 4)
                    ins = v.tensor_tensor(h[:, a + lo:a + lo + m, :],
                                          bank[:, 0:m * P].rearrange("p (t d) -> p t d", d=D),
                                          updb_bc[:, :].unsqueeze(1).broadcast_to([P, m, D]), ALU.add)
                    if lo + m < n:
                        flink(ins)
                    else:
                        ins.then_inc(new_ready, 1)
                v.wait_ge(act_done, k + 1)
                flink(v.tensor_tensor(h[:, a:b, :], h[:, a:b, :], xt[:, a:b, :], ALU.add))
                norm_stats(h, a, b, 2 * k)
                for t in range(a, b):
                    flink(v.tensor_scalar(y[:, t, :], h[:, t, :], mv[:, t, 0:1], rstd[:, t:t + 1],
                                          ALU.subtract, ALU.mult), wait=t == b - 1)
                flink(v.tensor_tensor(y[:, a:b, :], y[:, a:b, :],
                                      lnw_bc[:, :].unsqueeze(1).broadcast_to([P, n, D]), ALU.mult))
                flink(v.tensor_tensor(y[:, a:b, :], y[:, a:b, :], xb[:, a:b, :], ALU.add))
                norm_stats(y, a, b, 2 * k + 1)
                for t in range(a, b):
                    ins = v.tensor_scalar(y[:, t, :], y[:, t, :], mv[:, t, 0:1], rstd[:, t:t + 1],
                                          ALU.subtract, ALU.mult)
                    if t < b - 1:
                        flink(ins, wait=False)
                    else:
                        flink(ins)
                v.nop().then_inc(out_ready, 1)

            prepare(0)
            v.tensor_tensor(xb[:, :, :], xt[:, :, :], lnb_bc[:, :].unsqueeze(1).broadcast_to([P, TILES, D]),
                            ALU.add).then_inc(xb_done, 1)
            for what, a, b in SCHEDULE:
                if what == "slots":
                    if a < HEAVY_AT:
                        diags(PIECES[a][0], PIECES[b][0])
                elif what == "heavy":
                    heavy_rows()
                    diags(PIECES[HEAVY_AT][0], SEGS)
                else:
                    v.wait_ge(xb_done, 1)
                    finish(FINISHES.index((a, b)), a, b)

        @block.tensor
        def _(pe):
            pe.wait_ge(masks, 1)
            pe.wait_ge(w_in, 32)
            for n in range(4):
                src = wm if n < 2 else wu
                ins = pe.transpose(work(3)[:, n * P:(n + 1) * P], src[:, (n % 2) * D:(n % 2 + 1) * D], ident[:, :])
            ins.then_inc(wT_ps, 1)
            for k in range(BANKS):
                a, b = k * TPB, min((k + 1) * TPB, TILES)
                pe.wait_ge(x_in[k], 16)
                if b > FULL:
                    pe.wait_ge(xtail_in, 16)
                for t in range(a, b):
                    ins = pe.transpose(work(k)[:, (t - a) * P:(t - a + 1) * P], xt[:, t, :], ident[:, :])
                ins.then_inc(xT_ps, 1)
            pe.wait_ge(wT_ready, 1)
            for n, dst, done in ((1, None, d_ps), (0, work, s_ps)):
                for k in range(BANKS):
                    a, b = k * TPB, min((k + 1) * TPB, TILES)
                    pe.wait_ge(xT_ready[k], 1)
                    for t in range(a, b):
                        o = aggp[:, t * P:(t + 1) * P] if dst is None else dst(k)[:, (t - a) * P:(t - a + 1) * P]
                        ins = pe.matmul(o, xT[:, t * P:(t + 1) * P], wT[:, n, :], start=True, stop=True)
                    ins.then_inc(done, 1)
            for k in range(BANKS):
                w = min(BANK, NP - k * BANK)
                pe.wait_ge(d_ready, k + 1)
                pe.matmul(aggp[:, k * BANK:k * BANK + w], wT[:, 1, :], xT[:, k * BANK:k * BANK + w],
                          start=True, stop=True).then_inc(dT_ps, 1)
            pe.wait_ge(masks, 7)
            for k in range(BANKS):
                pe.wait_ge(dT_ready, k + 1)
                ins = pe.matmul(aggp[:, k * BANK:(k + 1) * BANK], zerob[0:1, 0:P], zerob[0:1, :],
                                start=True, stop=False, skip_group_check=True)
            ins.then_inc(agg_ready, 1)

            pe.wait_ge(heavy_ready, 1)
            pe.matmul(small[:, 0:TILES], below[:, :], heavy[:, :], start=True, stop=True)
            pe.matmul(small[:, 16:16 + TILES], ones16[:, :], heavy[:, :], start=True, stop=True)\
              .then_inc(places_ps, 1)
            pe.wait_ge(chunks_ready, 1)
            pe.wait_ge(s_ready, BANKS)

            def prepare(c):
                pe.wait_ge(id_rep_ready, c + 1)
                pe.matmul(small[:, 40:41], id_rep[:, :, :].rearrange("p a q -> p (a q)"),
                          ones32[:, 0:1], start=True, stop=True).then_inc(ids_ps, 1)
                pe.wait_ge(row_ix_ready, c + 1)
                for t in range(TILES):
                    ins = pe.matmul(small[:, P:P + CHUNK], s_rows[:, t, :], pick[:, t, :],
                                    start=(t == 0), stop=(t == TILES - 1))
                ins.then_inc(sTh_ps, 1)

            def heavy_rows():
                chunks = pe.value_load(counts[0:1, 0:1], min_val=1, max_val=MAX_CHUNKS)
                with pe.Fori(0, chunks) as c:
                    pe.wait_ge(parts_ready, c * SPLIT_STEPS + SPLIT_STEPS)
                    pe.sem_inc(passed, 1)
                    rows = pe.value_load(counts[0:1, 1:2], min_val=1, max_val=CHUNK)
                    with pe.Fori(0, rows) as r:
                        for k in range(2):
                            pe.wait_ge(half_used[k], c * CHUNK + r + 2)
                            for lo in range(0, HALF, BANK):
                                w = min(BANK, HALF - lo)
                                ins = pe.matmul(rowp[k][:, lo:lo + w], sel[:, bass.ds(r, 1)].broadcast_to([P, P]),
                                                part[:, k * HALF + lo:k * HALF + lo + w], start=True, stop=True)
                            ins.then_inc(rowp_ready[k], 1)
                    pe.wait_ge(aggh_ready, c + 1)
                    pe.transpose(small[0:CHUNK, 2 * P:3 * P], aggh[:, :], ident[:, :]).then_inc(agghT_ps, 1)
                    pe.wait_ge(agghT_ready, c + 1)
                    pe.wait_ge(spread_ready, c + 1)
                    for k in range(BANKS):
                        w = min(BANK, NP - k * BANK)
                        ins = pe.matmul(aggp[:, k * BANK:k * BANK + w], agghT[:, :], spread[:, k * BANK:k * BANK + w],
                                        start=False, stop=False, skip_group_check=True)
                    ins.then_inc(agg_ready, 1)
                    with pe.If(c + 1 < chunks):
                        prepare(c + 1)
                    pe.end_ifs()

            def slots(first, last):
                for p in range(first, last):
                    seg, lo, hi = PIECES[p]
                    t = TILE_OF_SEG[seg]
                    pe.wait_ge(gelu_done, p + 1)
                    pe.wait_ge(diag_ready, seg + 1)
                    for k in range(lo, hi):
                        ins = pe.matmul(aggp[:, t * P:(t + 1) * P], g[:, seg, k, :], diag[:, FIRST_SLOT[seg] + k, :],
                                        start=False, stop=(k == hi - 1), skip_group_check=True)
                    ins.then_inc(summed, 1)

            def finish(k, a, b):
                pe.wait_ge(aggS_ready, k + 1)
                for n in range(b - a):
                    t = a + n
                    bank = FIN_BANK[k] + n // TPB
                    if n % TPB == 0 and bank >= 4:
                        users = [m for m in range(k) if FIN_BANK[m] <= bank - 4]
                        pe.wait_ge(new_ready, users[-1] + 1)
                    o = work(bank % 4)[:, (n % TPB) * P:(n % TPB + 1) * P]
                    pe.matmul(o, aggS[:, t * P:(t + 1) * P], wT[:, 3, :], start=True, stop=False)
                    ins = pe.matmul(o, xT[:, t * P:(t + 1) * P], wT[:, 2, :], start=False, stop=True)
                ins.then_inc(new_ps, 1)

            prepare(0)
            for what, a, b in SCHEDULE:
                if what == "slots":
                    slots(a, b)
                elif what == "heavy":
                    heavy_rows()
                else:
                    finish(FINISHES.index((a, b)), a, b)


_INS = ['x', 'adj', 'L0_gnn_msg_w', 'L0_gnn_msg_b', 'L0_gnn_upd_w', 'L0_gnn_upd_b', 'L0_gnn_ln_w', 'L0_gnn_ln_b']


def kernel(**inputs):
    import concourse.bacc as _bacc
    from concourse.bass_utils import run_bass_kernel_spmd as _run

    nc = _bacc.Bacc("TRN2", target_bir_lowering=False, num_devices=1)
    arrays, args = {}, []
    for name in _INS:
        a = np.ascontiguousarray(inputs[name])
        arrays[f"in_{name}_dram"] = a
        args.append(nc.dram_tensor(f"in_{name}_dram", a.shape, mybir.dt.from_np(a.dtype), kind="ExternalInput").ap())
    shape = inputs["x"].shape
    out = nc.dram_tensor("out_0_dram", shape, F32, kind="ExternalOutput").ap()
    layer(nc, *args, out)
    r = _run(nc, [arrays], core_ids=[0])
    return r.results[0]["out_0_dram"]
```

```python
from contextlib import ExitStack

import numpy as np
import concourse.bass as bass
from concourse import mybir

F32 = mybir.dt.float32
BF16 = mybir.dt.bfloat16
F16 = mybir.dt.float16
I32 = mybir.dt.int32
U32 = mybir.dt.uint32
ALU = mybir.AluOpType
ACT = mybir.ActivationFunctionType
AX = mybir.AxisListType

P = 128
BANK = 512
SLOTS = 8
LN_EPS = 1e-5


def layer(nc, x, adj, msg_w, msg_b, upd_w, upd_b, ln_w, ln_b, out):
    N, D = x.shape
    TILES = -(-N // P)
    FULL = N // P
    TAIL = N - FULL * P
    NP = TILES * P
    SEGS_OF_TILE = [4, 2] + [1] * (TILES - 2)
    TILE_OF_SEG = [t for t in range(TILES) for _ in range(SEGS_OF_TILE[t])]
    SEGS = len(TILE_OF_SEG)
    FIRST_SEG = [TILE_OF_SEG.index(t) for t in range(TILES)]
    SPLIT_TILES = 2
    NC = -(-N // 4) * 4
    BANKS = -(-NP // BANK)
    TPB = BANK // P
    THIRDS = [(0, -(-N // 3)), (-(-N // 3), 2 * -(-N // 3)), (2 * -(-N // 3), N)]
    STREAMS = 3
    CHUNK = 32
    MAX_CHUNKS = -(-N // CHUNK)
    SLOTS_OF_SEG = [7 if t == 1 or t >= TILES - 3 else SLOTS for t in TILE_OF_SEG]
    FIRST_SLOT = [sum(SLOTS_OF_SEG[:seg]) for seg in range(SEGS + 1)]
    CUT = {SEGS_OF_TILE[0]: 5, SEGS - 1: 5}
    PIECES = [(seg, lo, hi) for seg in range(SEGS)
              for lo, hi in (((0, CUT[seg]), (CUT[seg], SLOTS_OF_SEG[seg])) if seg in CUT else ((0, SLOTS_OF_SEG[seg]),))]
    SEG_END = [max(p for p in range(len(PIECES)) if PIECES[p][0] == seg) + 1 for seg in range(SEGS)]
    LANDED = [16 * sum(b - a for _, a, b in PIECES[p % STREAMS:p + 1:STREAMS]) for p in range(len(PIECES))]
    assert FIRST_SLOT[SEGS] * P <= TILES * NC
    HEAVY_AT = SEG_END[SEGS_OF_TILE[0]] - 1
    FILLED_BY_V = (2, 3)
    EARLY_DIAGS = 3
    EARLY = 2
    GROUPS = [(0, 4), (4, 7), (7, 9), (9, 10), (10, 11)]
    NORMS = [(0, 4), (4, 7), (7, 9), (9, 11)]
    CENTRED = [sum(hi <= b for _, hi in GROUPS) for _, b in NORMS]
    MOMENTS = [n for k, m in enumerate(CENTRED) for n in (m + k, m + k + 1)]
    assert max(b - a for a, b in GROUPS) <= TPB
    GROUP_END = [SEG_END[FIRST_SEG[b - 1] + SEGS_OF_TILE[b - 1] - 1] for _, b in GROUPS]

    with ExitStack() as ctx:
        def sb(name, shape, dt):
            return ctx.enter_context(nc.sbuf_tensor(name, shape, dt))

        def pb(name, shape):
            return ctx.enter_context(nc.psum_tensor(name, shape, F32))

        def sem(name):
            return ctx.enter_context(nc.semaphore(name))

        xt = sb("xt", [P, TILES, D], F32)
        xT = sb("xT", [P, NP], F32)
        wm = sb("wm", [P, 2 * D], F32)
        wu = sb("wu", [P, 2 * D], F32)
        wT = sb("wT", [P, 4, D], F32)
        msgb_bc = sb("msgb_bc", [P, D], F32)
        updb = sb("updb", [1, D], F32)
        lnw_bc = sb("lnw_bc", [P, D], F32)
        lnb_bc = sb("lnb_bc", [P, D], F32)
        s_rows = sb("s_rows", [P, TILES, D], F32)
        d_rows = sb("d_rows", [P, TILES, D], F32)
        dT = sb("dT", [P, NP], F32)
        adj_sb = sb("adj_sb", [P, TILES, NC], F32)
        iota1 = sb("iota1", [P, NP], F32)
        ids = sb("ids", [P, TILES], F32)
        ident = sb("ident", [P, P], F32)
        identb = sb("identb", [P, P], BF16)
        below = sb("below", [P, P], F16)
        ones16 = sb("ones16", [P, P], F16)
        ones32 = sb("ones32", [P, TILES], F32)
        ones_row = sb("ones_row", [1, P], F32)
        sel = sb("sel", [P, CHUNK], BF16)
        zerob = sb("zerob", [1, BANK], BF16)
        top_w = sb("top_w", [P, SEGS, SLOTS], F32)
        top_j = sb("top_j", [P, SEGS * SLOTS], U32)
        g = sb("g", [P, FIRST_SLOT[SEGS], D], F32)
        diag = adj_sb[:, :, :].rearrange("p t n -> p (t n)")[:, 0:FIRST_SLOT[SEGS] * P].rearrange(
            "p (k q) -> p k q", q=P)
        nnz = sb("nnz", [P, TILES], F32)
        held = sb("held", [P, SEGS, SLOTS], F32)
        n_held = sb("n_held", [P, TILES], F32)
        heavy = sb("heavy", [P, TILES], F16)
        light = sb("light", [P, TILES], F32)
        upto = sb("upto", [P, TILES], F32)
        place = sb("place", [P, TILES], F32)
        left = sb("left", [1, 1], F32)
        chunk_start = sb("chunk_start", [1, MAX_CHUNKS], F32)
        over = sb("over", [1, MAX_CHUNKS], F32)
        n_chunks = sb("n_chunks", [1, 1], F32)
        pair_start = sb("pair_start", [1, CHUNK // 2], F32)
        pair_in = sb("pair_in", [1, CHUNK // 2], F32)
        pairs_f = sb("pairs_f", [1, 1], F32)
        counts = sb("counts", [1, 2], I32)
        pick = sb("pick", [P, TILES, CHUNK], F32)
        picked = sb("picked", [P, TILES, CHUNK], F32)
        id_sum = sb("id_sum", [P, CHUNK], F32)
        id_rep = sb("id_rep", [P, P // CHUNK, CHUNK], F32)
        spread = sb("spread", [P, NP], BF16)
        row_id = sb("row_id", [P, 1], F32)
        row_ix = sb("row_ix", [P, 1], I32)
        arow = sb("arow", [P, N], F32)
        part = sb("part", [P, N], BF16)
        sTh = sb("sTh", [P, CHUNK], F32)
        msg = sb("msg", [P, 2, N], F32)
        sum3 = sb("sum3", [P, 3, CHUNK], F32)
        aggh = sb("aggh", [P, P // CHUNK, CHUNK], F32)
        agghT = sb("agghT", [P, D], F32)
        agg_part = sb("agg_part", [P, D], BF16)
        aggS = sb("aggS", [P, NP], F32)
        h = d_rows
        xb = sb("xb", [P, TILES, D], F32)
        y = sb("y", [P, TILES, D], F32)
        stats = sb("stats", [P, TILES, 6], F32)
        mv = sb("mv", [P, TILES, 2], F32)
        eps = sb("eps", [P, 1], F32)
        sd = sb("sd", [P, TILES], F32)
        rstd = sb("rstd", [P, TILES], F32)

        aggp = pb("aggp", [P, BANKS * BANK])
        work_ps = pb("work_ps", [P, 4 * BANK])
        small = pb("small", [P, BANK])

        def work(k):
            return work_ps[:, k * BANK:(k + 1) * BANK]

        def new_bank(k):
            return work((k + 3) % 4)

        table = nc.dram_tensor("d_table", (NP, D), F32, kind="Internal").ap()

        passed = sem("passed")
        x_pad = sem("x_pad")
        adj_pad = sem("adj_pad")
        consts = sem("consts")
        masks = sem("masks")
        x_in = [sem(f"x_in{k}") for k in range(BANKS)]
        xtail_in = sem("xtail_in")
        wm_in = sem("wm_in")
        lnb_in = sem("lnb_in")
        wu_in = sem("wu_in")
        vec_in = sem("vec_in")
        adj_head = [sem(f"adj_head{t}") for t in range(SPLIT_TILES)]
        adj_in = [sem(f"adj_in{u}") for u in range(STREAMS)]
        xT_ps, wT_ps, d_ps, s_ps, dT_ps = (sem(n) for n in ("xT_ps", "wT_ps", "d_ps", "s_ps", "dT_ps"))
        wT_ready, d_ready, s_ready, dT_ready = (sem(n) for n in ("wT_ready", "d_ready", "s_ready", "dT_ready"))
        xT_ready = [sem(f"xT_ready{k}") for k in range(BANKS)]
        table_out = sem("table_out")
        xb_done = sem("xb_done")
        sel_half = sem("sel_half")
        starts_ready = sem("starts_ready")
        top_done = sem("top_done")
        found = sem("found")
        idx_ready = sem("idx_ready")
        cleared = sem("cleared")
        abs_done = sem("abs_done")
        nnz_ready = sem("nnz_ready")
        list_step = sem("list_step")
        heavy_ready = sem("heavy_ready")
        places_ps = sem("places_ps")
        chunks_ready = sem("chunks_ready")
        agg_ready = sem("agg_ready")
        chunk_step = sem("chunk_step")
        pair_step = sem("pair_step")
        pick_ready = sem("pick_ready")
        ids_ps = sem("ids_ps")
        sTh_ps = sem("sTh_ps")
        sTh_ready = sem("sTh_ready")
        row_ix_ready = sem("row_ix_ready")
        arow_in = sem("arow_in")
        parts_ready = sem("parts_ready")
        part1_ready = sem("part1_ready")
        msg_ready = sem("msg_ready")
        row_ps = [sem(f"row_ps{k}") for k in range(3)]
        third_used = [sem(f"third_used{k}") for k in range(3)]
        two_summed = sem("two_summed")
        aggh_ready = sem("aggh_ready")
        agghT_ps = sem("agghT_ps")
        spread_ready = sem("spread_ready")
        agg_split = sem("agg_split")
        agghT_ready = sem("agghT_ready")
        id_summed = sem("id_summed")
        id_rep_ready = sem("id_rep_ready")
        g_in = [sem(f"g_in{u}") for u in range(STREAMS)]
        prefilled = sem("prefilled")
        prefilled_v = sem("prefilled_v")
        gelu_done = sem("gelu_done")
        diag_ready = sem("diag_ready")
        summed = sem("summed")
        aggS_ready = sem("aggS_ready")
        new_ps = sem("new_ps")
        act_done = sem("act_done")
        fin_step = sem("fin_step")
        var_ready = sem("var_ready")
        sd_ready = sem("sd_ready")
        out_ready = sem("out_ready")
        stored = sem("stored")

        block = ctx.enter_context(nc.Block())
        PREP_STEPS, SPLIT_STEPS = 5, 5

        @block.sync
        def _(sp):
            for k in range(BANKS):
                a, b = k * TPB, min((k + 1) * TPB, FULL)
                sp.dma_start(xt[:, a:b, :], x[a * P:b * P, :].rearrange("(t p) d -> p t d", p=P)).then_inc(x_in[k], 16)
            sp.wait_ge(x_pad, 1)
            sp.dma_start(xt[0:TAIL, FULL, :], x[FULL * P:N, :]).then_inc(xtail_in, 16)
            for t in range(SPLIT_TILES):
                sp.dma_start(adj_sb[:, t, 0:N], adj[t * P:(t + 1) * P, :]).then_inc(adj_head[t], 16)
            sp.dma_start(wu[:, :], upd_w).then_inc(wu_in, 16)
            for row, vec in ((msgb_bc, msg_b), (lnw_bc, ln_w)):
                sp.dma_start(row[:, :], vec.partition_broadcast(P)).then_inc(vec_in, 16)
            sp.dma_start(updb[:, :], upd_b.partition_broadcast(1)).then_inc(vec_in, 16)
            for k in range(BANKS):
                sp.wait_ge(d_ready, k + 1)
                a, b = k * TPB, min((k + 1) * TPB, TILES)
                sp.dma_start(table[a * P:b * P, :].rearrange("(t p) d -> p t d", p=P),
                             d_rows[:, a:b, :]).then_inc(table_out, 16)
            for u in range(STREAMS):
                t = SPLIT_TILES + u
                sp.dma_start(adj_sb[:, t, 0:N], adj[t * P:(t + 1) * P, :]).then_inc(adj_in[u], 16)
            with sp.Fori(1, 2) as i:
                for u in range(STREAMS):
                    t = i * STREAMS + SPLIT_TILES + u
                    sp.wait_ge(adj_in[u], i * 16)
                    sp.dma_start(adj_sb[:, bass.ds(t, 1), 0:N].rearrange("p o n -> p (o n)"),
                                 adj[bass.ds(t * P, P), :]).then_inc(adj_in[u], 16)
            for u in range(STREAMS):
                t = SPLIT_TILES + 2 * STREAMS + u
                rows = min(P, N - t * P)
                sp.wait_ge(adj_in[u], 32)
                if rows < P:
                    sp.wait_ge(adj_pad, 2)
                sp.dma_start(adj_sb[0:rows, t, 0:N], adj[t * P:t * P + rows, :]).then_inc(adj_in[u], 16)
            n_out = 0
            for k, (a, b) in enumerate(NORMS):
                sp.wait_ge(out_ready, k + 1)
                f = min(b, FULL)
                if a < f:
                    sp.dma_start(out[a * P:f * P, :].rearrange("(t p) d -> p t d", p=P),
                                 y[:, a:f, :]).then_inc(stored, 16)
                    n_out += 1
                if b > FULL:
                    n_out += 1
            sp.wait_ge(stored, 16 * n_out)

        @block.gpsimd
        def _(pool):
            pool.iota(ids[:, :], [[P, TILES]], base=1, channel_multiplier=1,
                      allow_small_or_imprecise_dtypes=True).then_inc(consts, 1)
            for a, b in ((0, P), (P, NP)):
                pool.iota(iota1[:, a:b], [[1, b - a]], base=a + 1, channel_multiplier=0,
                          allow_small_or_imprecise_dtypes=True).then_inc(consts, 1)
            pool.wait_ge(table_out, 16 * BANKS)

            def gather(first, last):
                for p in range(first, last):
                    seg, lo, hi = PIECES[p]
                    u = p % STREAMS
                    pool.wait_ge(idx_ready, seg + 1)
                    if seg in FILLED_BY_V:
                        pool.wait_ge(prefilled_v, FILLED_BY_V.index(seg) + 1)
                    else:
                        pool.wait_ge(prefilled, seg + 1 - sum(n < seg for n in FILLED_BY_V))
                    if p >= STREAMS:
                        pool.wait_ge(g_in[u], LANDED[p - STREAMS])
                    for k in range(lo, hi):
                        n = seg * SLOTS + k
                        pool.indirect_dma_start(g[:, FIRST_SLOT[seg] + k, :], None, table,
                                                bass.IndirectOffsetOnAxis(top_j[:, n:n + 1], 0),
                                                compute_op=ALU.add).then_inc(g_in[u], 16)

            gather(0, HEAVY_AT)
            pool.wait_ge(chunks_ready, 1)
            chunks = pool.value_load(counts[0:1, 0:1], min_val=1, max_val=MAX_CHUNKS)
            with pool.Fori(0, chunks) as c:
                pool.wait_ge(row_ix_ready, c + 1)
                pool.sem_inc(passed, 1)
                pool.indirect_dma_start(arow[:, :], None, adj,
                                        bass.IndirectOffsetOnAxis(row_ix[:, 0:1], 0)).then_inc(arow_in, 16)
            gather(HEAVY_AT, len(PIECES))

        @block.scalar
        def _(act):
            act.dma_start(wm[:, :], msg_w).then_inc(wm_in, 16)
            act.dma_start(lnb_bc[:, :], ln_b.partition_broadcast(P)).then_inc(lnb_in, 16)
            for k in range(0, BANKS, 2):
                w = min(BANK, NP - k * BANK)
                act.wait_ge(xT_ps, k + 1)
                nc.scalar.copy(xT[:, k * BANK:k * BANK + w], work(k)[:, 0:w]).then_inc(xT_ready[k], 1)
            for k in range(BANKS):
                a, b = k * TPB, min((k + 1) * TPB, TILES)
                act.wait_ge(d_ps, k + 1)
                nc.scalar.copy(d_rows[:, a:b, :].rearrange("p t d -> p (t d)"),
                               aggp[:, a * P:b * P]).then_inc(d_ready, 1)
            act.preload_act_table(ACT.Gelu)

            def prefill(first, last):
                for seg in range(first, last):
                    t = TILE_OF_SEG[seg]
                    act.wait_ge(s_ready, t // TPB + 1)
                    nc.scalar.copy(g[:, FIRST_SLOT[seg]:FIRST_SLOT[seg + 1], :],
                                   s_rows[:, t, :].unsqueeze(1).broadcast_to(
                                       [P, SLOTS_OF_SEG[seg], D])).then_inc(prefilled, 1)

            scratch = [msg[:, 0, :], msg[:, 1, :], y[:, :, :].rearrange("p t d -> p (t d)")[:, 0:N]]

            def count(u, n, col):
                act.wait_ge(abs_done, n + 1)
                nc.scalar.activation(scratch[u], scratch[u], ACT.Sign, accum_out=col).then_inc(nnz_ready, 1)

            prefill(0, 2)
            for t in range(SPLIT_TILES):
                act.wait_ge(adj_head[t], 16)
                nc.scalar.activation(scratch[t], adj_sb[:, t, 0:N], ACT.Abs).then_inc(abs_done, 1)
            for t in range(SPLIT_TILES):
                count(t, t, nnz[:, t:t + 1])
            for k in range(BANKS):
                w = min(BANK, NP - k * BANK)
                act.wait_ge(dT_ps, k + 1)
                nc.scalar.copy(dT[:, k * BANK:k * BANK + w],
                               aggp[:, k * BANK:k * BANK + w]).then_inc(dT_ready, 1)
            act.wait_ge(nnz_ready, SPLIT_TILES)
            with act.Fori(0, (TILES - SPLIT_TILES) // STREAMS) as i:
                for u in range(STREAMS + 1):
                    t = i * STREAMS + SPLIT_TILES + u
                    if u < STREAMS:
                        act.wait_ge(adj_in[u], i * 16 + 16)
                        if u == 2:
                            act.wait_ge(adj_pad, 2)
                        if u == 0:
                            act.wait_ge(nnz_ready, t)
                            act.sem_inc(passed, 1)
                        nc.scalar.activation(scratch[u], adj_sb[:, bass.ds(t, 1), 0:N].rearrange("p o n -> p (o n)"),
                                             ACT.Abs).then_inc(abs_done, 1)
                    if u > 0:
                        act.wait_ge(abs_done, t)
                        act.sem_inc(passed, 1)
                        nc.scalar.activation(scratch[u - 1], scratch[u - 1], ACT.Sign,
                                             accum_out=nnz[:, bass.ds(t - 1, 1)]).then_inc(nnz_ready, 1)

            def slots(first, last):
                for p in range(first, last):
                    seg, lo, hi = PIECES[p]
                    act.wait_ge(g_in[p % STREAMS], LANDED[p])
                    gs = g[:, FIRST_SLOT[seg] + lo:FIRST_SLOT[seg] + hi, :].rearrange("p k d -> p (k d)")
                    nc.scalar.activation(gs, gs, ACT.Gelu).then_inc(gelu_done, 1)

            def prepare(c):
                act.wait_ge(sTh_ps, c + 1)
                nc.scalar.copy(sTh[:, :], work(0)[:, 0:CHUNK]).then_inc(sTh_ready, 1)

            def heavy_rows():
                chunks = act.value_load(counts[0:1, 0:1], min_val=1, max_val=MAX_CHUNKS)
                with act.Fori(0, chunks) as c:
                    second = slice(CHUNK, 2 * CHUNK)
                    act.wait_ge(parts_ready, c * SPLIT_STEPS + 2)
                    nc.scalar.copy(part[second, :], arow[second, :]).then_inc(part1_ready, 1)
                    act.wait_ge(sTh_ready, c + 1)
                    act.sem_inc(passed, 1)
                    pairs = act.value_load(counts[0:1, 1:2], min_val=1, max_val=CHUNK // 2)
                    with act.Fori(0, pairs) as q:
                        for e in range(2):
                            r = q * 2 + e
                            act.wait_ge(third_used[2], c * CHUNK + r + 1)
                            act.sem_inc(passed, 1)
                            nc.scalar.activation(msg[:, e, :], dT[:, 0:N], ACT.Gelu,
                                                 bias=sTh[:, bass.ds(r, 1)]).then_inc(msg_ready, 1)
                    with act.If(c + 1 < chunks):
                        prepare(c + 1)
                    act.end_ifs()

            def sums(k):
                a, b = GROUPS[k]
                act.wait_ge(summed, GROUP_END[k])
                nc.scalar.copy(aggS[:, a * P:b * P], aggp[:, a * P:b * P]).then_inc(aggS_ready, 1)

            def update(k):
                a, b = GROUPS[k]
                act.wait_ge(new_ps, k + 1)
                nc.scalar.activation(h[:, a:b, :].rearrange("p t d -> p (t d)"), new_bank(k)[:, 0:(b - a) * P],
                                     ACT.Gelu).then_inc(act_done, 1)

            def root(n):
                a, b = NORMS[n // 2]
                act.wait_ge(var_ready, MOMENTS[n])
                nc.scalar.activation(sd[:, a:b], mv[:, a:b, 1], ACT.Sqrt, bias=eps[:, 0:1]).then_inc(sd_ready, 1)

            prefill(FIRST_SEG[1], FIRST_SEG[1] + 3)
            slots(0, EARLY)
            prefill(FIRST_SEG[1] + 3, SEGS)
            prepare(0)
            act.wait_ge(nnz_ready, TILES)
            act.wait_ge(dT_ready, BANKS)
            act.wait_ge(masks, 9)
            act.wait_ge(chunks_ready, 1)
            slots(EARLY, HEAVY_AT)
            heavy_rows()
            slots(HEAVY_AT, GROUP_END[0] + 2)
            sums(0)
            update(0)
            slots(GROUP_END[0] + 2, GROUP_END[1])
            act.preload_act_table(ACT.Sqrt)
            root(0)
            sums(1)
            root(1)
            act.preload_act_table(ACT.Gelu)
            slots(GROUP_END[1], GROUP_END[1] + 1)
            update(1)
            slots(GROUP_END[1] + 1, GROUP_END[2])
            act.preload_act_table(ACT.Sqrt)
            root(2)
            sums(2)
            root(3)
            act.preload_act_table(ACT.Gelu)
            update(2)
            slots(GROUP_END[2], GROUP_END[3])
            act.preload_act_table(ACT.Sqrt)
            root(4)
            sums(3)
            root(5)
            act.preload_act_table(ACT.Gelu)
            slots(GROUP_END[3], GROUP_END[3] + 1)
            update(3)
            slots(GROUP_END[3] + 1, GROUP_END[4])
            sums(4)
            update(4)
            act.preload_act_table(ACT.Sqrt)
            root(6)
            root(7)
            act.wait_ge(out_ready, len(NORMS))
            act.dma_start(out[FULL * P:N, :], y[0:TAIL, FULL, :]).then_inc(stored, 16)

        @block.vector
        def _(v):
            v.memset(xt[TAIL // 32 * 32:P, FULL, :], 0.0).then_inc(x_pad, 1)
            v.memset(adj_sb[:, :, N:NC], 0.0).then_inc(adj_pad, 1)
            v.memset(adj_sb[TAIL // 32 * 32:P, FULL, 0:N], 0.0).then_inc(adj_pad, 1)
            v.wait_ge(consts, 2)
            q1 = iota1[:, 0:P]
            v.tensor_scalar(ident[:, :], q1, ids[:, 0:1], None, ALU.is_equal).then_inc(masks, 1)
            v.tensor_scalar(identb[:, :], q1, ids[:, 0:1], None, ALU.is_equal).then_inc(masks, 1)
            v.tensor_scalar(below[:, :], q1, ids[:, 0:1], None, ALU.is_gt).then_inc(masks, 1)
            v.memset(ones16[:, :], 1.0).then_inc(masks, 1)
            v.memset(ones32[:, :], 1.0).then_inc(masks, 1)
            v.memset(ones_row[:, :], 1.0).then_inc(masks, 1)
            v.memset(eps[:, :], LN_EPS).then_inc(masks, 1)
            v.memset(zerob[:, :], 0.0).then_inc(masks, 1)
            v.tensor_scalar(chunk_start[:, :], iota1[0:1, 0:MAX_CHUNKS], -1.0, float(CHUNK), ALU.add, ALU.mult)\
             .then_inc(starts_ready, 1)
            v.tensor_scalar(pair_start[:, :], iota1[0:1, 0:CHUNK // 2], -1.0, 2.0, ALU.add, ALU.mult)\
             .then_inc(starts_ready, 1)
            v.wait_ge(masks, 2)
            v.tensor_tensor(sel[:, :], identb[:, 0:CHUNK], identb[:, CHUNK:2 * CHUNK], ALU.add).then_inc(sel_half, 1)
            v.wait_ge(sel_half, 1)
            v.tensor_tensor(sel[:, :], sel[:, :], identb[:, 2 * CHUNK:3 * CHUNK], ALU.add).then_inc(masks, 1)

            def x_plus_b(k):
                a, b = k * TPB, min((k + 1) * TPB, TILES)
                v.wait_ge(x_in[k], 16)
                if b > FULL:
                    v.wait_ge(xtail_in, 16)
                v.tensor_tensor(xb[:, a:b, :], xt[:, a:b, :], lnb_bc[:, :].unsqueeze(1).broadcast_to([P, b - a, D]),
                                ALU.add).then_inc(xb_done, 1)

            v.wait_ge(lnb_in, 16)
            x_plus_b(0)
            v.wait_ge(wT_ps, 1)
            v.tensor_copy(wT[:, 0:2, :].rearrange("p a d -> p (a d)"), work(3)[:, 0:2 * P]).then_inc(wT_ready, 1)
            x_plus_b(1)
            v.wait_ge(xT_ps, 2)
            v.tensor_copy(xT[:, BANK:2 * BANK], work(1)).then_inc(xT_ready[1], 1)
            x_plus_b(2)

            n_found = 0

            def segment(seg):
                t = TILE_OF_SEG[seg]
                parts, q = SEGS_OF_TILE[t], seg - FIRST_SEG[t]
                if parts == 1:
                    return adj_sb[:, t, :], 1, 0
                return adj_sb[:, t, :].rearrange("p (n q) -> p q n", q=parts)[:, q, :], parts, q

            def largest(seg):
                t = TILE_OF_SEG[seg]
                turn, u = divmod(t - SPLIT_TILES, STREAMS)
                if t < SPLIT_TILES:
                    v.wait_ge(adj_head[t], 16)
                else:
                    v.wait_ge(adj_in[u], 16 * (turn + 1))
                if t == FULL:
                    v.wait_ge(adj_pad, 2)
                v.max(top_w[:, seg, :], segment(seg)[0]).then_inc(top_done, 1)

            def columns(seg):
                nonlocal n_found
                weights, step, first = segment(seg)
                tj = top_j[:, seg * SLOTS:(seg + 1) * SLOTS]
                v.wait_ge(top_done, seg + 1)
                ins = v.max_index(tj, top_w[:, seg, :], weights)
                if step == 1:
                    ins.then_inc(idx_ready, 1)
                else:
                    n_found += 1
                    ins.then_inc(found, 1)
                    v.wait_ge(found, n_found)
                    v.tensor_scalar(tj, tj, float(step), float(first), ALU.mult, ALU.add).then_inc(idx_ready, 1)

            v.wait_ge(adj_pad, 1)
            largest(0)
            for seg in range(SEGS):
                if seg + 1 < SEGS:
                    largest(seg + 1)
                columns(seg)
                k = seg - 2
                if 0 <= k < BANKS:
                    a, b = k * TPB, min((k + 1) * TPB, TILES)
                    if k == 0:
                        v.wait_ge(vec_in, 48)
                    v.wait_ge(s_ps, k + 1)
                    v.tensor_tensor(s_rows[:, a:b, :],
                                    work(k)[:, 0:(b - a) * P].rearrange("p (t d) -> p t d", d=D),
                                    msgb_bc[:, :].unsqueeze(1).broadcast_to([P, b - a, D]),
                                    ALU.add).then_inc(s_ready, 1)
                if k == BANKS:
                    v.wait_ge(wT_ps, 2)
                    v.tensor_copy(wT[:, 2:4, :].rearrange("p a d -> p (a d)"),
                                  work(3)[:, 2 * P:4 * P]).then_inc(wT_ready, 1)
                    v.wait_ge(s_ready, 1)
                    for n in FILLED_BY_V:
                        v.tensor_copy(g[:, FIRST_SLOT[n]:FIRST_SLOT[n + 1], :],
                                      s_rows[:, TILE_OF_SEG[n], :].unsqueeze(1).broadcast_to(
                                          [P, SLOTS_OF_SEG[n], D])).then_inc(prefilled_v, 1)
            v.wait_ge(idx_ready, SEGS)
            for seg in range(SEGS):
                if SLOTS_OF_SEG[seg] < SLOTS:
                    v.memset(top_w[:, seg, SLOTS_OF_SEG[seg]:SLOTS], 0.0).then_inc(cleared, 1)

            n_list = 0

            def link(ins):
                nonlocal n_list
                n_list += 1
                ins.then_inc(list_step, 1)
                v.wait_ge(list_step, n_list)

            v.wait_ge(cleared, sum(k < SLOTS for k in SLOTS_OF_SEG))
            link(v.tensor_scalar(held[:, :, :], top_w[:, :, :], 0.0, None, ALU.is_gt))
            for t in range(SPLIT_TILES):
                a, b = FIRST_SEG[t], FIRST_SEG[t] + SEGS_OF_TILE[t]
                v.tensor_reduce(n_held[:, t:t + 1], held[:, a:b, :].rearrange("p s k -> p (s k)"),
                                AX.X, ALU.add).then_inc(list_step, 1)
                n_list += 1
            link(v.tensor_reduce(n_held[:, SPLIT_TILES:TILES], held[:, FIRST_SEG[SPLIT_TILES]:SEGS, :],
                                 AX.X, ALU.add))
            v.wait_ge(nnz_ready, TILES)
            v.tensor_tensor(heavy[:, :], nnz[:, :], n_held[:, :], ALU.not_equal).then_inc(heavy_ready, 1)
            link(v.tensor_tensor(light[:, :], nnz[:, :], n_held[:, :], ALU.is_equal))
            for t in range(SPLIT_TILES):
                tw = top_w[:, FIRST_SEG[t]:FIRST_SEG[t] + SEGS_OF_TILE[t], :]
                v.tensor_scalar(tw, tw, light[:, t:t + 1], None, ALU.mult).then_inc(list_step, 1)
                n_list += 1
            v.wait_ge(heavy_ready, 1)
            v.wait_ge(starts_ready, 2)
            v.wait_ge(places_ps, 1)
            within, total = small[:, 0:TILES], small[:, 16:16 + TILES]
            link(v.tensor_tensor_scan(upto[:, :], ones32[:, :], total, 0.0, ALU.mult, ALU.add))
            v.tensor_scalar(over[:, :], chunk_start[:, :], upto[0:1, TILES - 1:TILES], None,
                            ALU.is_lt).then_inc(list_step, 1)
            n_list += 1
            v.tensor_copy(left[:, :], upto[0:1, TILES - 1:TILES]).then_inc(list_step, 1)
            n_list += 1
            link(v.tensor_tensor(place[:, :], upto[:, :], total, ALU.subtract))
            v.tensor_reduce(n_chunks[:, :], over[:, :], AX.X, ALU.add).then_inc(list_step, 1)
            n_list += 1
            link(v.scalar_tensor_tensor(place[:, :], place[:, :], 1.0, within, ALU.add, ALU.add))
            v.tensor_scalar(counts[0:1, 0:1], n_chunks[:, :], 1.0, None, ALU.max).then_inc(chunks_ready, 1)
            link(v.tensor_tensor(place[:, :], place[:, :], heavy[:, :], ALU.mult))
            v.wait_ge(s_ready, BANKS)
            v.wait_ge(consts, 3)
            for k in range(3):
                v.sem_inc(third_used[k], 2)

            def prepare(c):
                base = c * PREP_STEPS
                v.wait_ge(agg_ready, c + 1)
                v.tensor_tensor(pick[:, :, :], place[:, :].unsqueeze(2).broadcast_to([P, TILES, CHUNK]),
                                iota1[:, 0:CHUNK].unsqueeze(1).broadcast_to([P, TILES, CHUNK]),
                                ALU.is_equal).then_inc(pick_ready, 1)
                v.memset(sum3[:, :, :], 0.0).then_inc(chunk_step, 1)
                v.wait_ge(pick_ready, c + 1)
                v.tensor_tensor(picked[:, :, :], pick[:, :, :],
                                ids[:, :].unsqueeze(2).broadcast_to([P, TILES, CHUNK]), ALU.mult).then_inc(chunk_step, 1)
                v.wait_ge(chunk_step, base + 2)
                v.tensor_reduce(id_sum[:, :], picked[:, :, :].rearrange("p t q -> p q t"),
                                AX.X, ALU.add).then_inc(id_summed, 1)
                v.wait_ge(id_summed, c + 1)
                v.tensor_copy(id_rep[:, :, :], id_sum[:, :].unsqueeze(1).broadcast_to(
                    [P, P // CHUNK, CHUNK])).then_inc(id_rep_ready, 1)
                v.tensor_scalar(place[:, :], place[:, :], -float(CHUNK), None, ALU.add).then_inc(chunk_step, 1)
                v.tensor_scalar(pair_in[:, :], pair_start[:, :], left[0:1, 0:1], None, ALU.is_lt).then_inc(pair_step, 1)
                v.wait_ge(pair_step, c * 3 + 1)
                v.tensor_scalar(left[:, :], left[:, :], -float(CHUNK), None, ALU.add).then_inc(pair_step, 1)
                v.tensor_reduce(pairs_f[:, :], pair_in[:, :], AX.X, ALU.add).then_inc(pair_step, 1)
                v.wait_ge(pair_step, c * 3 + 3)
                v.tensor_scalar(counts[0:1, 1:2], pairs_f[:, :], 1.0, None, ALU.max).then_inc(chunk_step, 1)
                v.wait_ge(ids_ps, c + 1)
                v.tensor_copy(row_id[:, :], small[:, 40:41]).then_inc(chunk_step, 1)
                v.tensor_scalar(row_ix[:, :], small[:, 40:41], -1.0, 0.0, ALU.add, ALU.max).then_inc(row_ix_ready, 1)

            def heavy_rows():
                chunks = v.value_load(counts[0:1, 0:1], min_val=1, max_val=MAX_CHUNKS)
                with v.Fori(0, chunks) as c:
                    base = c * SPLIT_STEPS
                    two = slice(2 * CHUNK, P)
                    v.wait_ge(chunk_step, c * PREP_STEPS + PREP_STEPS)
                    v.sem_inc(passed, 1)
                    pairs = v.value_load(counts[0:1, 1:2], min_val=1, max_val=CHUNK // 2)
                    v.tensor_scalar(spread[:, :], iota1[:, :], row_id[:, 0:1], None,
                                    ALU.is_equal).then_inc(spread_ready, 1)
                    v.wait_ge(arow_in, c * 16 + 16)
                    v.tensor_copy(part[:, :], arow[:, :]).then_inc(parts_ready, 1)
                    v.wait_ge(parts_ready, base + 1)
                    v.tensor_tensor(arow[:, :], arow[:, :], part[:, :], ALU.subtract).then_inc(parts_ready, 1)
                    v.wait_ge(parts_ready, base + 2)
                    v.tensor_copy(part[two, :], arow[two, :]).then_inc(parts_ready, 1)
                    v.wait_ge(parts_ready, base + 3)
                    v.tensor_tensor(part[two, :], arow[two, :], part[two, :], ALU.subtract).then_inc(parts_ready, 1)
                    v.wait_ge(part1_ready, c + 1)
                    v.wait_ge(parts_ready, base + 4)
                    v.sem_inc(parts_ready, 1)
                    with v.Fori(0, pairs) as q:
                        for e in range(2):
                            r = q * 2 + e
                            v.wait_ge(msg_ready, c * CHUNK + r + 1)
                            for k, (lo, hi) in enumerate(THIRDS):
                                v.wait_ge(row_ps[k], c * CHUNK + r + 1)
                                v.scalar_tensor_tensor(msg[:, e, lo:hi], msg[:, e, lo:hi], 1.0, work(k)[:, 0:hi - lo],
                                                       ALU.mult, ALU.mult,
                                                       accum_out=sum3[:, k, bass.ds(r, 1)]).then_inc(third_used[k], 1)
                    for k in range(3):
                        v.wait_ge(third_used[k], c * CHUNK + pairs * 2 + 2)
                    v.tensor_tensor(sum3[:, 0, :], sum3[:, 0, :], sum3[:, 1, :], ALU.add).then_inc(two_summed, 1)
                    v.wait_ge(two_summed, c + 1)
                    v.tensor_tensor(aggh[:, :, :], sum3[:, 0:1, :].broadcast_to([P, P // CHUNK, CHUNK]),
                                    sum3[:, 2:3, :].broadcast_to([P, P // CHUNK, CHUNK]), ALU.add).then_inc(aggh_ready, 1)
                    v.wait_ge(agghT_ps, c + 1)
                    sums = small[:, 2 * P:3 * P]
                    v.tensor_copy(agg_part[:, :], sums).then_inc(agg_split, 1)
                    v.wait_ge(agg_split, c * 4 + 1)
                    v.tensor_tensor(agghT[:, :], sums, agg_part[:, :], ALU.subtract).then_inc(agg_split, 1)
                    v.wait_ge(agg_split, c * 4 + 2)
                    v.tensor_copy(agg_part[two, :], agghT[two, :]).then_inc(agg_split, 1)
                    v.tensor_copy(agg_part[CHUNK:2 * CHUNK, :], agghT[CHUNK:2 * CHUNK, :]).then_inc(agg_split, 1)
                    v.wait_ge(agg_split, c * 4 + 4)
                    v.tensor_tensor(agg_part[two, :], agghT[two, :], agg_part[two, :],
                                    ALU.subtract).then_inc(agghT_ready, 1)
                    with v.If(c + 1 < chunks):
                        prepare(c + 1)
                    v.end_ifs()

            def diags(first, last):
                for seg in range(first, last):
                    n = SLOTS_OF_SEG[seg]
                    v.tensor_tensor(diag[:, FIRST_SLOT[seg]:FIRST_SLOT[seg] + n, :],
                                    ident[:, :].unsqueeze(1).broadcast_to([P, n, P]),
                                    top_w[:, seg, 0:n].unsqueeze(2).broadcast_to([P, n, P]),
                                    ALU.mult).then_inc(diag_ready, 1)

            n_fin = 0

            def flink(ins, wait=True):
                nonlocal n_fin
                n_fin += 1
                ins.then_inc(fin_step, 1)
                if wait:
                    v.wait_ge(fin_step, n_fin)

            def moments(src, a, b):
                for t in range(a, b):
                    flink(v.bn_stats(stats[:, t, :], src[:, t, :]), wait=t == b - 1)
                for t in range(a, b):
                    ins = v.bn_aggr(mv[:, t, :], stats[:, t, :])
                    if t < b - 1:
                        flink(ins, wait=False)
                ins.then_inc(var_ready, 1)

            def inverse(a, b, n):
                v.wait_ge(sd_ready, n + 1)
                flink(v.reciprocal(rstd[:, a:b], sd[:, a:b]))

            def centre(k):
                a, b = GROUPS[k]
                v.wait_ge(act_done, k + 1)
                flink(v.tensor_tensor(h[:, a:b, :], h[:, a:b, :], xt[:, a:b, :], ALU.add))
                moments(h, a, b)
                v.wait_ge(var_ready, k + 1 + sum(hi <= a for _, hi in NORMS))
                for t in range(a, b):
                    flink(v.scalar_tensor_tensor(y[:, t, :], h[:, t, :], mv[:, t, 0:1], lnw_bc[:, :],
                                                 ALU.subtract, ALU.mult), wait=False)

            def norms(k):
                a, b = NORMS[k]
                inverse(a, b, 2 * k)
                for t in range(a, b):
                    flink(v.scalar_tensor_tensor(y[:, t, :], y[:, t, :], rstd[:, t:t + 1], xb[:, t, :],
                                                 ALU.mult, ALU.add), wait=t == b - 1)
                moments(y, a, b)
                v.wait_ge(var_ready, MOMENTS[2 * k + 1])
                inverse(a, b, 2 * k + 1)
                for t in range(a, b):
                    flink(v.tensor_scalar(y[:, t, :], y[:, t, :], mv[:, t, 0:1], rstd[:, t:t + 1],
                                          ALU.subtract, ALU.mult), wait=t == b - 1)
                v.nop().then_inc(out_ready, 1)

            prepare(0)
            tw = top_w[:, FIRST_SEG[SPLIT_TILES]:SEGS, :]
            link(v.tensor_tensor(tw, tw, light[:, SPLIT_TILES:TILES].unsqueeze(2).broadcast_to(
                [P, TILES - SPLIT_TILES, SLOTS]), ALU.mult))
            v.wait_ge(chunks_ready, 1)
            diags(0, EARLY_DIAGS)
            heavy_rows()
            diags(EARLY_DIAGS, SEGS)
            v.wait_ge(xb_done, BANKS)
            for k in range(len(NORMS)):
                for m in range(CENTRED[k - 1] if k else 0, CENTRED[k]):
                    centre(m)
                norms(k)

        @block.tensor
        def _(pe):
            pe.wait_ge(masks, 1)

            def transpose_w(n):
                src = (wm, wu)[n]
                pe.wait_ge((wm_in, wu_in)[n], 16)
                for m in range(2):
                    ins = pe.transpose(work(3)[:, (2 * n + m) * P:(2 * n + m + 1) * P], src[:, m * D:(m + 1) * D],
                                       ident[:, :])
                ins.then_inc(wT_ps, 1)

            def transpose_x(k):
                a, b = k * TPB, min((k + 1) * TPB, TILES)
                pe.wait_ge(x_in[k], 16)
                if b > FULL:
                    pe.wait_ge(xtail_in, 16)
                for t in range(a, b):
                    ins = pe.transpose(work(k)[:, (t - a) * P:(t - a + 1) * P], xt[:, t, :], ident[:, :])
                ins.then_inc(xT_ps, 1)

            def features(n, k, dst, done):
                pe.wait_ge(wT_ready, 1)
                pe.wait_ge(xT_ready[k], 1)
                a, b = k * TPB, min((k + 1) * TPB, TILES)
                for t in range(a, b):
                    ins = pe.matmul(dst[:, (t - a) * P:(t - a + 1) * P], xT[:, t * P:(t + 1) * P], wT[:, n, :],
                                    start=True, stop=True)
                ins.then_inc(done, 1)

            transpose_x(0)
            transpose_w(0)
            for k in range(1, BANKS):
                transpose_x(k)
            for k in range(BANKS):
                features(1, k, aggp[:, k * BANK:(k + 1) * BANK], d_ps)
            transpose_w(1)
            for k in range(BANKS):
                features(0, k, work(k), s_ps)
            for k in range(BANKS):
                w = min(BANK, NP - k * BANK)
                pe.wait_ge(d_ready, k + 1)
                pe.matmul(aggp[:, k * BANK:k * BANK + w], wT[:, 1, :], xT[:, k * BANK:k * BANK + w],
                          start=True, stop=True).then_inc(dT_ps, 1)
            pe.wait_ge(masks, 9)
            for k in range(BANKS):
                pe.wait_ge(dT_ready, k + 1)
                ins = pe.matmul(aggp[:, k * BANK:(k + 1) * BANK], zerob[0:1, 0:P], zerob[0:1, :],
                                start=True, stop=False, skip_group_check=True)
            ins.then_inc(agg_ready, 1)

            def new_start(k):
                a, b = GROUPS[k]
                if k >= 4:
                    pe.wait_ge(act_done, k - 3)
                pe.matmul(new_bank(k)[:, 0:(b - a) * P], ones_row[0:1, :],
                          updb[0:1, :].unsqueeze(1).broadcast_to([1, b - a, D]),
                          start=True, stop=False, skip_group_check=True)
                for t in range(a, b):
                    pe.matmul(new_bank(k)[:, (t - a) * P:(t - a + 1) * P], xT[:, t * P:(t + 1) * P], wT[:, 2, :],
                              start=False, stop=False, skip_group_check=True)

            pe.wait_ge(wT_ready, 2)
            pe.wait_ge(vec_in, 48)
            new_start(0)

            pe.wait_ge(heavy_ready, 1)
            pe.matmul(small[:, 0:TILES], below[:, :], heavy[:, :], start=True, stop=True)
            pe.matmul(small[:, 16:16 + TILES], ones16[:, :], heavy[:, :], start=True, stop=True)\
              .then_inc(places_ps, 1)
            pe.wait_ge(s_ready, BANKS)

            def prepare(c):
                pe.wait_ge(id_rep_ready, c + 1)
                pe.matmul(small[:, 40:41], id_rep[:, :, :].rearrange("p a q -> p (a q)"),
                          ones32[:, 0:1], start=True, stop=True).then_inc(ids_ps, 1)
                for t in range(TILES):
                    ins = pe.matmul(work(0)[:, 0:CHUNK], s_rows[:, t, :], pick[:, t, :],
                                    start=(t == 0), stop=(t == TILES - 1))
                ins.then_inc(sTh_ps, 1)

            def heavy_rows():
                pe.wait_ge(chunks_ready, 1)
                chunks = pe.value_load(counts[0:1, 0:1], min_val=1, max_val=MAX_CHUNKS)
                with pe.Fori(0, chunks) as c:
                    pe.wait_ge(chunk_step, c * PREP_STEPS + PREP_STEPS)
                    pe.sem_inc(passed, 1)
                    pairs = pe.value_load(counts[0:1, 1:2], min_val=1, max_val=CHUNK // 2)
                    pe.wait_ge(sTh_ready, c + 1)
                    pe.wait_ge(parts_ready, c * SPLIT_STEPS + SPLIT_STEPS)
                    pe.sem_inc(passed, 1)
                    with pe.Fori(0, pairs) as q:
                        for e in range(2):
                            r = q * 2 + e
                            for k, (lo, hi) in enumerate(THIRDS):
                                pe.wait_ge(third_used[k], c * CHUNK + r + 2)
                                pe.matmul(work(k)[:, 0:hi - lo], sel[:, bass.ds(r, 1)].broadcast_to([P, P]),
                                          part[:, lo:hi], start=True, stop=True).then_inc(row_ps[k], 1)
                    pe.wait_ge(aggh_ready, c + 1)
                    pe.transpose(small[:, 2 * P:3 * P], aggh[:, :, :].rearrange("p a q -> p (a q)"),
                                 ident[:, :]).then_inc(agghT_ps, 1)
                    pe.wait_ge(agghT_ready, c + 1)
                    pe.wait_ge(spread_ready, c + 1)
                    for k in range(BANKS):
                        w = min(BANK, NP - k * BANK)
                        ins = pe.matmul(aggp[:, k * BANK:k * BANK + w], agg_part[0:3 * CHUNK, :],
                                        spread[0:3 * CHUNK, k * BANK:k * BANK + w],
                                        start=False, stop=False, skip_group_check=True)
                    ins.then_inc(agg_ready, 1)
                    with pe.If(c + 1 < chunks):
                        prepare(c + 1)
                    pe.end_ifs()

            def slots(first, last):
                for p in range(first, last):
                    seg, lo, hi = PIECES[p]
                    t = TILE_OF_SEG[seg]
                    pe.wait_ge(gelu_done, p + 1)
                    pe.wait_ge(diag_ready, seg + 1)
                    for k in range(lo, hi):
                        n = FIRST_SLOT[seg] + k
                        ins = pe.matmul(aggp[:, t * P:(t + 1) * P], g[:, n, :], diag[:, n, :],
                                        start=False, stop=(k == hi - 1), skip_group_check=True)
                    ins.then_inc(summed, 1)

            def new_end(k):
                pe.wait_ge(aggS_ready, k + 1)
                a, b = GROUPS[k]
                for t in range(a, b):
                    ins = pe.matmul(new_bank(k)[:, (t - a) * P:(t - a + 1) * P], aggS[:, t * P:(t + 1) * P], wT[:, 3, :],
                                    start=False, stop=True, skip_group_check=True)
                ins.then_inc(new_ps, 1)

            prepare(0)
            slots(0, EARLY)
            heavy_rows()
            slots(EARLY, GROUP_END[0])
            new_end(0)
            slots(GROUP_END[0], GROUP_END[1])
            new_start(1)
            new_end(1)
            for k in range(2, len(GROUPS)):
                new_start(k)
            for k in range(2, len(GROUPS)):
                slots(GROUP_END[k - 1], GROUP_END[k])
                new_end(k)


_INS = ['x', 'adj', 'L0_gnn_msg_w', 'L0_gnn_msg_b', 'L0_gnn_upd_w', 'L0_gnn_upd_b', 'L0_gnn_ln_w', 'L0_gnn_ln_b']


def kernel(**inputs):
    import concourse.bacc as _bacc
    from concourse.bass_utils import run_bass_kernel_spmd as _run

    nc = _bacc.Bacc("TRN2", target_bir_lowering=False, num_devices=1)
    arrays, args = {}, []
    for name in _INS:
        a = np.ascontiguousarray(inputs[name])
        arrays[f"in_{name}_dram"] = a
        args.append(nc.dram_tensor(f"in_{name}_dram", a.shape, mybir.dt.from_np(a.dtype), kind="ExternalInput").ap())
    shape = inputs["x"].shape
    out = nc.dram_tensor("out_0_dram", shape, F32, kind="ExternalOutput").ap()
    layer(nc, *args, out)
    r = _run(nc, [arrays], core_ids=[0])
    return r.results[0]["out_0_dram"]
```
